# Optimizing a Trainium2 kernel written in Bass

```python
import numpy as np
import jax
import jax.numpy as jnp

def _softmax(x, axis=-1):
    return jax.nn.softmax(x, axis=axis)

def _gelu(x):
    return jax.nn.gelu(x, approximate=True)

def _silu(x):
    return jax.nn.silu(x)

def _sigmoid(x):
    return jax.nn.sigmoid(x)

def _layernorm(x, axis=-1, eps=1e-05):
    m = jnp.mean(x, axis=axis, keepdims=True)
    v = jnp.var(x, axis=axis, keepdims=True)
    return (x - m) / jnp.sqrt(v + eps)

def _scatter_add(tgt, idx, src, axis=0):
    return tgt.at[idx].add(src)

def _segment_sum(src, seg, n):
    return jax.ops.segment_sum(src, seg, n)
kernel_name = 'mk_xattn_seq_d2_seqx_r8_e0452c'

def setup_inputs(seed: int=0):
    np.random.seed(seed)
    _w = jnp.asarray

    def _rec_inputs():
        import jax
        import jax.numpy as jnp
        _rk = jax.random.key(seed)
        x = -0.0002928 + 1 * jax.random.normal(jax.random.fold_in(_rk, 1), (16, 128, 128), jnp.float32)
        _lenS = 128 - jax.random.randint(jax.random.fold_in(_rk, 7), (16,), 0, max(1, 128 // 4) + 1, jnp.int32)
        _lenS2 = 128 - jax.random.randint(jax.random.fold_in(_rk, 8), (16,), 0, max(1, 128 // 4) + 1, jnp.int32)
        _ctx_1024P = jax.random.normal(jax.random.fold_in(_rk, 11), (16, 16, 128), jnp.float32)
        _ctx_1024c = jax.random.dirichlet(jax.random.fold_in(_rk, 511), 0.3 * jnp.ones((16,), jnp.float32), (16, 128))
        _ctx_1024t = jnp.einsum('bsk,bkd->bsd', _ctx_1024c, _ctx_1024P)
        _ctx_1024t = _ctx_1024t * jax.lax.rsqrt(jnp.mean(jnp.square(_ctx_1024t)) + 1e-12) * 0.953939
        ctx_1024 = -1.39393e-06 + 0.999914 * (_ctx_1024t + 0.3 * jax.random.normal(jax.random.fold_in(_rk, 611), (16, 128, 128), jnp.float32))
        return (x, ctx_1024)
    x, ctx_1024 = _rec_inputs()

    def _L0_xattn_setup():
        import jax, jax.numpy as jnp
        import numpy as np
        EPS = 1e-05

        def _layernorm(x, g, b):
            m = jnp.mean(x, axis=-1, keepdims=True)
            v = jnp.mean((x - m) ** 2, axis=-1, keepdims=True)
            return (x - m) / jnp.sqrt(v + EPS) * g + b

        def _mha(x, kv, Wq, Wk, Wv, mask, causal):
            m = mask[:, None]
            Q = jnp.einsum('bsd,hdk->bhsk', x, Wq) * m
            K = jnp.einsum('bsd,hdk->bhsk', kv, Wk) * m
            V = jnp.einsum('bsd,hdk->bhsk', kv, Wv) * m
            energy = jnp.einsum('bhsk,bhtk->bhst', Q, K)
            S = energy.shape[-1]
            lengths = jnp.sum(energy[:, :, 0, :] != 0, axis=-1)
            cols = jnp.arange(S)
            energy = jnp.where(cols[None, None, None, :] >= lengths[:, :, None, None], -jnp.inf, energy)
            if causal:
                energy = jnp.where(cols[None, :] > cols[:, None], -jnp.inf, energy)
            dk = Wq.shape[-1]
            score = jax.nn.softmax(energy / jnp.sqrt(jnp.asarray(dk, energy.dtype)), axis=-1)
            out = jnp.einsum('bhst,bhtk->bhsk', score, V) * m
            B, H, Sx, dkk = out.shape
            return out.transpose(0, 2, 1, 3).reshape(B, Sx, H * dkk)
        key = jax.random.key(seed)
        ks = jax.random.split(key, 20)
        B, S, D, H = (2, 256, 128, 16)
        dk = D // H
        sd = 0.02
        inp = {'x': jax.random.normal(ks[0], (B, S, D), jnp.float32), 'context': jax.random.normal(ks[1], (B, S, D), jnp.float32), 'Wq1': jax.random.normal(ks[2], (H, D, dk), jnp.float32) * sd, 'Wk1': jax.random.normal(ks[3], (H, D, dk), jnp.float32) * sd, 'Wv1': jax.random.normal(ks[4], (H, D, dk), jnp.float32) * sd, 'Wq2': jax.random.normal(ks[5], (H, D, dk), jnp.float32) * sd, 'Wk2': jax.random.normal(ks[6], (H, D, dk), jnp.float32) * sd, 'Wv2': jax.random.normal(ks[7], (H, D, dk), jnp.float32) * sd, 'ln1_g': jnp.ones((D,), jnp.float32), 'ln1_b': jnp.zeros((D,), jnp.float32), 'ln2_g': jnp.ones((D,), jnp.float32), 'ln2_b': jnp.zeros((D,), jnp.float32), 'ln3_g': jnp.ones((D,), jnp.float32), 'ln3_b': jnp.zeros((D,), jnp.float32), 'fc1_w': jax.random.normal(ks[8], (D, D), jnp.float32) * sd, 'fc1_b': jnp.zeros((D,), jnp.float32), 'fc2_w': jax.random.normal(ks[9], (D, D), jnp.float32) * sd, 'fc2_b': jnp.zeros((D,), jnp.float32)}
        return inp
    _L0_xattn_all = _L0_xattn_setup()
    _L0_xattn_in = {k: v for k, v in _L0_xattn_all.items() if k in ('Wq1', 'Wk1', 'Wv1', 'Wq2', 'Wk2', 'Wv2', 'ln1_g', 'ln1_b', 'ln2_g', 'ln2_b', 'ln3_g', 'ln3_b', 'fc1_w', 'fc1_b', 'fc2_w', 'fc2_b')}
    del _L0_xattn_all

    def _L1_xattn_setup():
        import jax, jax.numpy as jnp
        import numpy as np
        D_MODEL = 128
        N_HEADS = 16
        D_K = D_MODEL // N_HEADS
        LN_EPS = 1e-05

        def _attention(query, key_value, W_qkv, b_qkv, W_o, b_o, ln_gamma, ln_beta):
            B, Sq, _ = query.shape
            Skv = key_value.shape[1]
            Wq, Wk, Wv = (W_qkv[:D_MODEL], W_qkv[D_MODEL:2 * D_MODEL], W_qkv[2 * D_MODEL:])
            bq, bk, bv = (b_qkv[:D_MODEL], b_qkv[D_MODEL:2 * D_MODEL], b_qkv[2 * D_MODEL:])
            Q = (query @ Wq.T + bq).reshape(B, Sq, N_HEADS, D_K).transpose(0, 2, 1, 3)
            K = (key_value @ Wk.T + bk).reshape(B, Skv, N_HEADS, D_K).transpose(0, 2, 1, 3)
            V = (key_value @ Wv.T + bv).reshape(B, Skv, N_HEADS, D_K).transpose(0, 2, 1, 3)
            scores = jnp.einsum('bhqd,bhkd->bhqk', Q.astype(jnp.float32), K.astype(jnp.float32))
            scores = scores / np.sqrt(D_K)
            attn = jax.nn.softmax(scores, axis=-1)
            context = jnp.einsum('bhqk,bhkd->bhqd', attn, V.astype(jnp.float32)).astype(query.dtype)
            context = context.transpose(0, 2, 1, 3).reshape(B, Sq, D_MODEL)
            output = context @ W_o.T + b_o
            x = output + query
            mu = jnp.mean(x, axis=-1, keepdims=True)
            var = jnp.mean(jnp.square(x - mu), axis=-1, keepdims=True)
            return (x - mu) / jnp.sqrt(var + LN_EPS) * ln_gamma + ln_beta
        key = jax.random.key(seed)
        ks = jax.random.split(key, 8)
        B, Sq, Skv = (2, 256, 256)
        scale = 1.0 / np.sqrt(D_MODEL)
        return {'query': jax.random.normal(ks[0], (B, Sq, D_MODEL), dtype=jnp.float32), 'key_value': jax.random.normal(ks[1], (B, Skv, D_MODEL), dtype=jnp.float32), 'W_qkv': jax.random.normal(ks[2], (3 * D_MODEL, D_MODEL), dtype=jnp.float32) * scale, 'b_qkv': jax.random.normal(ks[3], (3 * D_MODEL,), dtype=jnp.float32) * 0.01, 'W_o': jax.random.normal(ks[4], (D_MODEL, D_MODEL), dtype=jnp.float32) * scale, 'b_o': jax.random.normal(ks[5], (D_MODEL,), dtype=jnp.float32) * 0.01, 'ln_gamma': jnp.ones((D_MODEL,), dtype=jnp.float32), 'ln_beta': jnp.zeros((D_MODEL,), dtype=jnp.float32)}
    _L1_xattn_all = _L1_xattn_setup()
    _L1_xattn_in = {k: v for k, v in _L1_xattn_all.items() if k in ('W_qkv', 'b_qkv', 'W_o', 'b_o', 'ln_gamma', 'ln_beta')}
    del _L1_xattn_all
    return {'x': x, 'ctx_1024': ctx_1024, 'L0_xattn_Wq1': _L0_xattn_in['Wq1'], 'L0_xattn_Wk1': _L0_xattn_in['Wk1'], 'L0_xattn_Wv1': _L0_xattn_in['Wv1'], 'L0_xattn_Wq2': _L0_xattn_in['Wq2'], 'L0_xattn_Wk2': _L0_xattn_in['Wk2'], 'L0_xattn_Wv2': _L0_xattn_in['Wv2'], 'L0_xattn_ln1_g': _L0_xattn_in['ln1_g'], 'L0_xattn_ln1_b': _L0_xattn_in['ln1_b'], 'L0_xattn_ln2_g': _L0_xattn_in['ln2_g'], 'L0_xattn_ln2_b': _L0_xattn_in['ln2_b'], 'L0_xattn_ln3_g': _L0_xattn_in['ln3_g'], 'L0_xattn_ln3_b': _L0_xattn_in['ln3_b'], 'L0_xattn_fc1_w': _L0_xattn_in['fc1_w'], 'L0_xattn_fc1_b': _L0_xattn_in['fc1_b'], 'L0_xattn_fc2_w': _L0_xattn_in['fc2_w'], 'L0_xattn_fc2_b': _L0_xattn_in['fc2_b'], 'L1_xattn_W_qkv': _L1_xattn_in['W_qkv'], 'L1_xattn_b_qkv': _L1_xattn_in['b_qkv'], 'L1_xattn_W_o': _L1_xattn_in['W_o'], 'L1_xattn_b_o': _L1_xattn_in['b_o'], 'L1_xattn_ln_gamma': _L1_xattn_in['ln_gamma'], 'L1_xattn_ln_beta': _L1_xattn_in['ln_beta']}

def reference(x, ctx_1024, L0_xattn_Wq1, L0_xattn_Wk1, L0_xattn_Wv1, L0_xattn_Wq2, L0_xattn_Wk2, L0_xattn_Wv2, L0_xattn_ln1_g, L0_xattn_ln1_b, L0_xattn_ln2_g, L0_xattn_ln2_b, L0_xattn_ln3_g, L0_xattn_ln3_b, L0_xattn_fc1_w, L0_xattn_fc1_b, L0_xattn_fc2_w, L0_xattn_fc2_b, L1_xattn_W_qkv, L1_xattn_b_qkv, L1_xattn_W_o, L1_xattn_b_o, L1_xattn_ln_gamma, L1_xattn_ln_beta):
    import jax
    import jax.numpy as jnp

    def _L0_xattn_ref(x, context, Wq1, Wk1, Wv1, Wq2, Wk2, Wv2, ln1_g, ln1_b, ln2_g, ln2_b, ln3_g, ln3_b, fc1_w, fc1_b, fc2_w, fc2_b):
        import jax, jax.numpy as jnp
        import numpy as np
        EPS = 1e-05

        def _layernorm(x, g, b):
            m = jnp.mean(x, axis=-1, keepdims=True)
            v = jnp.mean((x - m) ** 2, axis=-1, keepdims=True)
            return (x - m) / jnp.sqrt(v + EPS) * g + b

        def _mha(x, kv, Wq, Wk, Wv, mask, causal):
            m = mask[:, None]
            Q = jnp.einsum('bsd,hdk->bhsk', x, Wq) * m
            K = jnp.einsum('bsd,hdk->bhsk', kv, Wk) * m
            V = jnp.einsum('bsd,hdk->bhsk', kv, Wv) * m
            energy = jnp.einsum('bhsk,bhtk->bhst', Q, K)
            S = energy.shape[-1]
            lengths = jnp.sum(energy[:, :, 0, :] != 0, axis=-1)
            cols = jnp.arange(S)
            energy = jnp.where(cols[None, None, None, :] >= lengths[:, :, None, None], -jnp.inf, energy)
            if causal:
                energy = jnp.where(cols[None, :] > cols[:, None], -jnp.inf, energy)
            dk = Wq.shape[-1]
            score = jax.nn.softmax(energy / jnp.sqrt(jnp.asarray(dk, energy.dtype)), axis=-1)
            out = jnp.einsum('bhst,bhtk->bhsk', score, V) * m
            B, H, Sx, dkk = out.shape
            return out.transpose(0, 2, 1, 3).reshape(B, Sx, H * dkk)
        mask0 = 1.0 - jnp.all(x == 0, axis=2, keepdims=True).astype(x.dtype)
        z = _mha(x, x, Wq1, Wk1, Wv1, mask0, causal=True)
        x1 = _layernorm(x + z, ln1_g, ln1_b)
        mask1 = 1.0 - jnp.all(x1 == 0, axis=2, keepdims=True).astype(x1.dtype)
        z = _mha(x1, context, Wq2, Wk2, Wv2, mask1, causal=False)
        x2 = _layernorm(x1 + z, ln2_g, ln2_b)
        z = jnp.maximum(x2 @ fc1_w.T + fc1_b, 0.0) * mask0
        z = (z @ fc2_w.T + fc2_b) * mask0
        return _layernorm(x2 + z, ln3_g, ln3_b)

    def _L1_xattn_ref(query, key_value, W_qkv, b_qkv, W_o, b_o, ln_gamma, ln_beta):
        import jax, jax.numpy as jnp
        import numpy as np
        D_MODEL = 128
        N_HEADS = 16
        D_K = D_MODEL // N_HEADS
        LN_EPS = 1e-05

        def _attention(query, key_value, W_qkv, b_qkv, W_o, b_o, ln_gamma, ln_beta):
            B, Sq, _ = query.shape
            Skv = key_value.shape[1]
            Wq, Wk, Wv = (W_qkv[:D_MODEL], W_qkv[D_MODEL:2 * D_MODEL], W_qkv[2 * D_MODEL:])
            bq, bk, bv = (b_qkv[:D_MODEL], b_qkv[D_MODEL:2 * D_MODEL], b_qkv[2 * D_MODEL:])
            Q = (query @ Wq.T + bq).reshape(B, Sq, N_HEADS, D_K).transpose(0, 2, 1, 3)
            K = (key_value @ Wk.T + bk).reshape(B, Skv, N_HEADS, D_K).transpose(0, 2, 1, 3)
            V = (key_value @ Wv.T + bv).reshape(B, Skv, N_HEADS, D_K).transpose(0, 2, 1, 3)
            scores = jnp.einsum('bhqd,bhkd->bhqk', Q.astype(jnp.float32), K.astype(jnp.float32))
            scores = scores / np.sqrt(D_K)
            attn = jax.nn.softmax(scores, axis=-1)
            context = jnp.einsum('bhqk,bhkd->bhqd', attn, V.astype(jnp.float32)).astype(query.dtype)
            context = context.transpose(0, 2, 1, 3).reshape(B, Sq, D_MODEL)
            output = context @ W_o.T + b_o
            x = output + query
            mu = jnp.mean(x, axis=-1, keepdims=True)
            var = jnp.mean(jnp.square(x - mu), axis=-1, keepdims=True)
            return (x - mu) / jnp.sqrt(var + LN_EPS) * ln_gamma + ln_beta
        return _attention(query, key_value, W_qkv, b_qkv, W_o, b_o, ln_gamma, ln_beta)
    x = _L0_xattn_ref(x, ctx_1024, L0_xattn_Wq1, L0_xattn_Wk1, L0_xattn_Wv1, L0_xattn_Wq2, L0_xattn_Wk2, L0_xattn_Wv2, L0_xattn_ln1_g, L0_xattn_ln1_b, L0_xattn_ln2_g, L0_xattn_ln2_b, L0_xattn_ln3_g, L0_xattn_ln3_b, L0_xattn_fc1_w, L0_xattn_fc1_b, L0_xattn_fc2_w, L0_xattn_fc2_b)
    x = _L1_xattn_ref(x, ctx_1024, L1_xattn_W_qkv, L1_xattn_b_qkv, L1_xattn_W_o, L1_xattn_b_o, L1_xattn_ln_gamma, L1_xattn_ln_beta)
    return x

_drawn_inputs = setup_inputs


def setup_inputs(seed=0):
    import zlib

    import numpy as np

    out = dict(_drawn_inputs(seed))
    spreads = {'L0_xattn_ln1_g': (1.0, 0.2),
     'L0_xattn_ln1_b': (0.0, 0.1),
     'L0_xattn_ln2_g': (1.0, 0.2),
     'L0_xattn_ln2_b': (0.0, 0.1),
     'L0_xattn_ln3_g': (1.0, 0.2),
     'L0_xattn_ln3_b': (0.0, 0.1),
     'L0_xattn_fc1_b': (0.0, 0.726),
     'L0_xattn_fc2_b': (0.0, 0.1),
     'L1_xattn_ln_gamma': (1.0, 0.2),
     'L1_xattn_ln_beta': (0.0, 0.1)}
    factors = {'L0_xattn_Wq1': 8.0,
     'L0_xattn_Wk1': 8.0,
     'L0_xattn_Wq2': 8.0,
     'L0_xattn_Wk2': 8.0,
     'L1_xattn_b_qkv': 8.0,
     'L1_xattn_b_o': 5.856}
    for name, (base, spread) in spreads.items():
        noise = np.random.default_rng([zlib.crc32(name.encode()), seed]).standard_normal(out[name].shape)
        drawn = base * np.exp(spread * noise) if base else spread * noise
        out[name] = jnp.asarray(drawn.astype(out[name].dtype))
    for name, factor in factors.items():
        out[name] = (out[name] * factor).astype(out[name].dtype)
    return out
```

```python
from contextlib import ExitStack

import concourse.bass as bass
from concourse import mybir

F32 = mybir.dt.float32
F32R = mybir.dt.float32r
BF16 = mybir.dt.bfloat16
ALU = mybir.AluOpType
ACT = mybir.ActivationFunctionType
AX_X = mybir.AxisListType.X

B, S, D, H = 16, 128, 128, 16
DK = D // H
BLOCKS = 4
QUADS = H // BLOCKS
ROWS = 128 // BLOCKS
TERMS = 3
DATA = TERMS * DK
NEGMAX_ROW, SLEN_ROW, TLEN_ROW = DATA, DATA + 2, DATA + 3
SLOTS = 4
SELF, CROSS, OUTER = range(3)
LAYERS = 3
PERIOD = SLOTS * LAYERS
UNITS = B * LAYERS
LOAD_AHEAD = 5
AHEAD = 3
BIG = 1.0e30
EPS = 1e-5
WQ, WK, WV = ([0, 3, 6], [1, 4, 7], [2, 5, 8])
WO, FC1, FC2 = 9, 10, 11
N_WEIGHTS = 12
LN1G, LN1B, LN2G, LN2B, LN3G, LN3B, FC2B, GAMMA, BETA, BO, BV = range(11)
N_ROWS = 11


class Event:

    def __init__(self, sem, per, step=1, slot=None):
        self.sem, self.per, self.step, self.slot = sem, per, step, slot

    def upto(self, r):
        return sum(self.per.get(v // SLOTS, 0) for v in range(r)
                   if self.slot is None or v % SLOTS == self.slot)

    def __call__(self, unit, k=None):
        turn, n = unit
        full, r = divmod(n, PERIOD)
        per = self.per.get(r // SLOTS, 0)
        if self.slot is not None and r % SLOTS != self.slot:
            per = 0
        count = full * self.upto(PERIOD) + self.upto(r) + (per if k is None else k)
        if turn is None:
            return max(count, 0) * self.step
        return turn * (self.upto(PERIOD) * self.step) + count * self.step


def layer_of(unit):
    return unit[1] % PERIOD // SLOTS


def slot_of(unit):
    return unit[1] % SLOTS


def plus(unit, n):
    return unit[0], unit[1] + n


def exists(unit):
    return unit[0] is not None or 0 <= unit[1] < UNITS


def run_steps(eng, step, first, last):
    head = first + PERIOD
    turns = (last - head) // PERIOD
    for n in range(first, head):
        step((None, n))
    with eng.Fori(0, turns) as turn:
        for n in range(head, head + PERIOD):
            step((turn, n))
    for n in range(head + turns * PERIOD, last):
        step((None, n))


def xattn_kernel(nc, x, ctx_in, weights, rows, qk_bias, fc1_bias, out):
    with ExitStack() as stack:
        def sb(name, shape, dt=F32):
            return stack.enter_context(nc.sbuf_tensor(name, shape, dt))

        def bank(name):
            return stack.enter_context(nc.psum_tensor(name, [128, 512], F32))

        def sem(name):
            return stack.enter_context(nc.semaphore(name))

        def event(name, per, step=1, slot=None):
            if isinstance(per, int):
                per = {l: per for l in range(LAYERS)}
            return Event(sem(name), per, step, slot)

        def slot_events(name, per, step=16):
            return [event(f"{name}{b}", per, step, b) for b in range(SLOTS)]

        w_sb = sb("w_sb", [128, N_WEIGHTS, D])
        rows_sb = sb("rows_sb", [128, N_ROWS, D])
        qk_bias_sb = sb("qk_bias_sb", [1, 2, D])
        fc1_bias_sb = sb("fc1_bias_sb", [128, 1])
        w_packed = sb("w_packed", [128, 2 * LAYERS, QUADS, BLOCKS, ROWS])
        bias_row = sb("bias_row", [1, 4, QUADS, BLOCKS, ROWS])
        one_sb = sb("one_sb", [1, 1])
        bias_col = sb("bias_col", [128, 4, QUADS])
        ident = sb("ident", [128, 128])
        ident_r = sb("ident_r", [128, 128], F32R)
        ident_b = sb("ident_b", [128, 128], BF16)
        future_s = sb("future_s", [128, 128], BF16)
        future_t = sb("future_t", [128, 128], BF16)
        iota_t = sb("iota_t", [128, 128])
        block_mask = sb("block_mask", [128, BLOCKS])
        low_rows = sb("low_rows", [128, 2])
        low_row = sb("low_row", [1, 2, BLOCKS, ROWS])
        zero_rows = sb("zero_rows", [H, 128], F32R)

        x_in = sb("x_in", [128, SLOTS, D])
        ctx = sb("ctx", [128, SLOTS, D])
        ctx_m = sb("ctx_m", [128, D])
        x1 = sb("x1", [128, SLOTS, D])
        x2 = sb("x2", [128, SLOTS, D])
        x3 = sb("x3", [128, SLOTS, D])
        mask0 = sb("mask0", [128, SLOTS])
        mask1 = sb("mask1", [128, SLOTS])
        count = sb("count", [128, 1])
        junk = sb("junk", [128, 128])
        xc_T = sb("xc_T", [128, 2, 128])
        biased = sb("biased", [128, 2, QUADS, S])
        low_hi = sb("low_hi", [128, 2, QUADS, S], F32R)
        packed = sb("packed", [128, SLOTS, 2, QUADS, S], F32R)
        spread = sb("spread", [128, SLOTS, 2, BLOCKS, QUADS, S], F32R)
        first_q = sb("first_q", [128, QUADS, ROWS])
        length = sb("length", [128, 1])
        len_inverse = sb("len_inverse", [128, 1])
        len_big = sb("len_big", [128, 1])
        len_mask = sb("len_mask", [128, S], F32R)
        v_aug = sb("v_aug", [128, SLOTS, H, ROWS])
        negmax = sb("negmax", [128, H])
        negmax_parts = sb("negmax_parts", [128, 2, H], F32R)
        negmax_T = sb("negmax_T", [2 * H, S], F32R)
        probs = sb("probs", [128, 4, BLOCKS * S])
        o_sb = sb("o_sb", [128, QUADS, S])
        recip = sb("recip", [128, H])
        z = sb("z", [128, D])
        y = sb("y", [128, D])
        stats = sb("stats", [128, 6])
        mean_var = sb("mean_var", [128, 2])
        bubble = sb("bubble", [128, 1])
        var_eps = sb("var_eps", [128, 1])
        var_eps2 = sb("var_eps2", [128, 1])
        minus_half = sb("minus_half", [128, 1])
        rstd = sb("rstd", [128, 1])
        xn = sb("xn", [128, D])
        scaled = sb("scaled", [128, D])
        ctx_v = sb("ctx_v", [128, D])
        tail_res = sb("tail_res", [128, 2, D])
        tail_T = sb("tail_T", [128, 128])
        hidden_T = sb("hidden_T", [128, 128])
        y2 = sb("y2", [128, D])
        stats2 = sb("stats2", [128, 6])
        mean_var2 = sb("mean_var2", [128, 2])
        rstd2 = sb("rstd2", [128, 1])
        xn2 = sb("xn2", [128, D])
        scaled2 = sb("scaled2", [128, D])
        y_out = sb("y_out", [128, 2, D])
        len_dram = nc.dram_tensor("len_dram", (SLOTS, 128, S), F32, kind="Internal").ap()

        score_bank = [bank("score0"), bank("score1")]
        attend_bank = [bank("attend0"), bank("attend1")]
        o_bank = bank("o_bank")
        t_bank = bank("t_bank")
        q_bank = bank("q_bank")
        k_bank = bank("k_bank")
        x_T_ps, c_T_ps = t_bank[:, 0:128], t_bank[:, 128:256]
        v_ps = t_bank[:, 256:384]
        nm_T_ps = t_bank[0:2 * H, 384:512]

        weights_in = sem("weights_in")
        rows_in = sem("rows_in")
        pool_setup = sem("pool_setup")
        pool_zeros = sem("pool_zeros")
        dve_setup = sem("dve_setup")
        zeroed = [sem(f"zeroed{b}") for b in range(SLOTS)]
        bias_ps = sem("bias_ps")
        bias_done = sem("bias_done")
        x_loaded = slot_events("x_loaded", {SELF: 1})
        ctx_loaded = slot_events("ctx_loaded", {SELF: 1})
        spread_done = slot_events("spread_done", BLOCKS)
        negmax_done = slot_events("negmax_done", 1)
        len_stored = slot_events("len_stored", {SELF: 1, CROSS: 1})
        len_done = slot_events("len_done", {SELF: 2, CROSS: 2, OUTER: 1})
        out_stored = slot_events("out_stored", {OUTER: 1})
        x_T_done = event("x_T_done", 1)
        q_done = event("q_done", 1)
        k_done = event("k_done", 1)
        v_done = event("v_done", 1)
        first_done = event("first_done", {SELF: 1, CROSS: 1})
        scored = event("scored", QUADS)
        nm_T_done = event("nm_T_done", 1)
        attended = event("attended", QUADS)
        pv_done = event("pv_done", QUADS)
        o_T_done = event("o_T_done", 1)
        tail_T_done = event("tail_T_done", {CROSS: 1, OUTER: 1})
        tail_1_done = event("tail_1_done", {CROSS: 1, OUTER: 1})
        tail_2_done = event("tail_2_done", {CROSS: 1})
        xc_T_ready = event("xc_T_ready", 1)
        low_hi_q = event("low_hi_q", 1)
        low_hi_k = event("low_hi_k", 1)
        v_ready = event("v_ready", 1)
        negmax_T_ready = event("negmax_T_ready", 1)
        exp_done = event("exp_done", QUADS)
        o_ready = event("o_ready", 1)
        tail_T_ready = event("tail_T_ready", {CROSS: 1, OUTER: 1})
        hidden_ready = event("hidden_ready", {CROSS: 1})
        prep = event("prep", {SELF: 2, CROSS: 3})
        biased_done = event("biased_done", {OUTER: 2})
        packed_q = event("packed_q", 1)
        packed_k = event("packed_k", 1)
        first_ready = event("first_ready", {SELF: 1, CROSS: 1})
        len_chain = event("len_chain", {SELF: 4, CROSS: 4})
        max_done = event("max_done", QUADS)
        parts_chain = event("parts_chain", 2)
        norm = event("norm", {SELF: 7, CROSS: 7, OUTER: 2})
        tail_norm = event("tail_norm", {CROSS: 6, OUTER: 5})
        rstd_ready = event("rstd_ready", {SELF: 1, CROSS: 1})
        rstd2_ready = event("rstd2_ready", {CROSS: 1, OUTER: 1})
        x1_chain = event("x1_chain", {SELF: 2})
        x2_chain = event("x2_chain", {CROSS: 2})
        ctx_v_ready = event("ctx_v_ready", {OUTER: 1})
        outer_res_ready = event("outer_res_ready", {OUTER: 1})
        x3_chain = event("x3_chain", {CROSS: 2})
        y_chain = event("y_chain", {OUTER: 2})

        block = stack.enter_context(nc.Block())

        def quad_before(unit, q, n):
            return plus(unit, (q - n) // QUADS), (q - n) % QUADS + 1

        N_POOL_SETUP, N_DVE_SETUP = 19, 6

        @block.tensor
        def _(pe):
            def front_transpose(f):
                if not exists(f):
                    return
                l, b = layer_of(f), slot_of(f)
                pe.wait_ge(v_ready.sem, v_ready(plus(f, -1)))
                if l == SELF:
                    pe.wait_ge(x_loaded[b].sem, x_loaded[b](f))
                    nc.tensor.transpose(x_T_ps, x_in[:, b, :], ident[:, :]).then_inc(x_T_done.sem, 1)
                    return
                if l == CROSS:
                    pe.wait_ge(prep.sem, prep(f))
                    pe.wait_ge(x1_chain.sem, x1_chain(plus(f, -SLOTS)))
                else:
                    pe.wait_ge(ctx_loaded[b].sem, ctx_loaded[b](f))
                    pe.wait_ge(x3_chain.sem, x3_chain(plus(f, -SLOTS)))
                nc.tensor.transpose(c_T_ps, ctx_m[:, :] if l == CROSS else ctx[:, b, :], ident[:, :])
                nc.tensor.transpose(x_T_ps, (x1 if l == CROSS else x3)[:, b, :],
                                    ident[:, :]).then_inc(x_T_done.sem, 1)

            def project(f, kind):
                if not exists(f):
                    return
                l = layer_of(f)
                pe.wait_ge(xc_T_ready.sem, xc_T_ready(f))
                if kind == 0:
                    pe.wait_ge(tail_norm.sem, tail_norm(plus(f, -AHEAD - 1)))
                    pe.wait_ge(packed_q.sem, packed_q(plus(f, -1)))
                else:
                    pe.wait_ge(packed_k.sem, packed_k(plus(f, -1)))
                    pe.wait_ge(len_chain.sem, len_chain(plus(f, -1)))
                src = xc_T[:, 1 if kind and l != SELF else 0, :]
                dst = k_bank if kind else q_bank
                for q in range(QUADS):
                    last = nc.tensor.matmul(dst[:, q * S:(q + 1) * S], w_packed[:, 2 * l + kind, q, :, :],
                                            src, start=True, stop=True)
                last.then_inc((k_done if kind else q_done).sem, 1)

            def project_v(f):
                if not exists(f):
                    return
                l = layer_of(f)
                pe.wait_ge(negmax_T_ready.sem, negmax_T_ready(plus(f, 1 - AHEAD)))
                nc.tensor.matmul(v_ps, xc_T[:, 0 if l == SELF else 1, :], w_sb[:, WV[l], :],
                                 start=True, stop=True).then_inc(v_done.sem, 1)

            def first_scores(f):
                if not exists(f) or layer_of(f) == OUTER:
                    return
                pe.wait_ge(first_ready.sem, first_ready(f))
                for q in range(QUADS):
                    last = nc.tensor.matmul(k_bank[32 * q:32 * q + 32, 0:S], first_q[:, q, :],
                                            packed[:, slot_of(f), 1, q, :].bitcast(F32), start=True, stop=True)
                last.then_inc(first_done.sem, 1)

            def score(u, q):
                if not exists(u):
                    return
                b, causal = slot_of(u), layer_of(u) == SELF
                if q == 0:
                    pe.wait_ge(spread_done[b].sem, spread_done[b](u))
                    pe.wait_ge(len_done[b].sem, len_done[b](u))
                pe.wait_ge(max_done.sem, max_done(*quad_before(u, q, 2)))
                dst = score_bank[q % 2]
                last = nc.tensor.matmul(dst[:, :], packed[:, b, 0, q, :], spread[:, b, 1, :, q, :],
                                        start=True, stop=not causal)
                if causal:
                    last = nc.tensor.matmul(dst[:, :], ident_b[:, :],
                                            future_s[:, :].unsqueeze(1).broadcast_to([128, BLOCKS, S]),
                                            start=False, stop=True)
                last.then_inc(scored.sem, 1)

            def transpose_negmax(u):
                if not exists(u):
                    return
                pe.wait_ge(parts_chain.sem, parts_chain(u))
                pe.wait_ge(xc_T_ready.sem, xc_T_ready(plus(u, AHEAD - 1) if exists(plus(u, AHEAD - 1)) else (None, UNITS - 1)))
                pe.wait_ge(v_ready.sem, v_ready(plus(u, AHEAD - 2) if exists(plus(u, AHEAD - 2)) else (None, UNITS - 1)))
                nc.tensor.transpose(nm_T_ps.bitcast(F32R), negmax_parts[:, :, :].rearrange("p a h -> p (a h)"),
                                    ident_r[:, :]).then_inc(nm_T_done.sem, 1)

            def attend(u, q):
                if not exists(u):
                    return
                b, causal = slot_of(u), layer_of(u) == SELF
                if q == 0:
                    pe.wait_ge(negmax_done[b].sem, negmax_done[b](u))
                pe.wait_ge(exp_done.sem, exp_done(*quad_before(u, q, 2)))
                dst = attend_bank[q % 2]
                last = nc.tensor.matmul(dst[:, :], packed[:, b, 1, q, :], spread[:, b, 0, :, q, :],
                                        start=True, stop=not causal)
                if causal:
                    last = nc.tensor.matmul(dst[:, :], ident_b[:, :],
                                            future_t[:, :].unsqueeze(1).broadcast_to([128, BLOCKS, S]),
                                            start=False, stop=True)
                last.then_inc(attended.sem, 1)

            def values(u, q):
                if not exists(u):
                    return
                if q == 0:
                    pe.wait_ge(v_ready.sem, v_ready(u))
                    pe.wait_ge(norm.sem, norm(plus(u, -1), 2))
                pe.wait_ge(exp_done.sem, exp_done(u, q + 1))
                for j in range(BLOCKS):
                    last = nc.tensor.matmul(o_bank[32 * j:32 * j + 32, q * S:(q + 1) * S],
                                            v_aug[:, slot_of(u), BLOCKS * j + q, :],
                                            probs[:, q, j * S:(j + 1) * S], start=True, stop=True)
                last.then_inc(pv_done.sem, 1)

            def transpose_o(u):
                if not exists(u):
                    return
                pe.wait_ge(o_ready.sem, o_ready(u))
                for q in range(QUADS):
                    last = nc.tensor.transpose(o_bank[:, q * S:(q + 1) * S], o_sb[:, q, :], ident[:, :])
                last.then_inc(o_T_done.sem, 1)

            def tail(w, part):
                if not exists(w) or layer_of(w) == SELF or (part == 2 and layer_of(w) == OUTER):
                    return
                l, b = layer_of(w), slot_of(w)
                if part == 0:
                    g = plus(w, AHEAD)
                    g = g if exists(g) else (None, UNITS - 1)
                    pe.wait_ge(packed_q.sem, packed_q(g))
                    if l == CROSS:
                        pe.wait_ge(x2_chain.sem, x2_chain(w))
                    else:
                        pe.wait_ge(ctx_v_ready.sem, ctx_v_ready(w))
                    nc.tensor.transpose(q_bank[:, 0:128], x2[:, b, :] if l == CROSS else ctx_v[:, :],
                                        ident[:, :]).then_inc(tail_T_done.sem, 1)
                elif part == 1:
                    pe.wait_ge(tail_T_ready.sem, tail_T_ready(w))
                    if l == CROSS:
                        mm = nc.tensor.matmul(q_bank[:, 128:256], w_sb[:, FC1, :], tail_T[:, :],
                                              start=True, stop=True)
                    else:
                        mm = nc.tensor.matmul(q_bank[:, 128:256], tail_T[:, :], w_sb[:, WO, :],
                                              start=True, stop=True)
                    mm.then_inc(tail_1_done.sem, 1)
                else:
                    pe.wait_ge(hidden_ready.sem, hidden_ready(w))
                    nc.tensor.matmul(q_bank[:, 256:384], hidden_T[:, :], w_sb[:, FC2, :],
                                     start=True, stop=True).then_inc(tail_2_done.sem, 1)

            def step(u):
                front, ahead = plus(u, AHEAD), plus(u, 1)
                tail(plus(u, -1), 0)
                score(ahead, 0)
                attend(u, 2)
                values(u, 1)
                tail(plus(u, -1), 1)
                score(ahead, 1)
                attend(u, 3)
                values(u, 2)
                tail(plus(u, -1), 2)
                score(ahead, 2)
                values(u, 3)
                score(ahead, 3)
                front_transpose(front)
                transpose_o(u)
                project(front, 0)
                transpose_negmax(ahead)
                project(front, 1)
                project_v(front)
                attend(ahead, 0)
                first_scores(front)
                attend(ahead, 1)
                values(ahead, 0)

            pe.wait_ge(weights_in, 16)
            pe.wait_ge(pool_setup, N_POOL_SETUP)
            pe.wait_ge(dve_setup, N_DVE_SETUP)
            for kind in range(4):
                for q in range(QUADS):
                    last = nc.tensor.matmul(k_bank[:, QUADS * kind + q:QUADS * kind + q + 1],
                                            bias_row[0:1, kind, q, :, :], one_sb[:, :], start=True, stop=True)
            for kind in range(2):
                last = nc.tensor.matmul(k_bank[:, 4 * QUADS + kind:4 * QUADS + kind + 1],
                                        low_row[0:1, kind, :, :], one_sb[:, :], start=True, stop=True)
            last.then_inc(bias_ps, 1)
            pe.wait_ge(bias_done, 2)
            run_steps(pe, step, -LOAD_AHEAD, UNITS + 1)

        @block.scalar
        def _(act):
            def tail_evac(w, part):
                if not exists(w) or layer_of(w) == SELF or (part == 1 and layer_of(w) == OUTER):
                    return
                if part == 0:
                    act.wait_ge(tail_T_done.sem, tail_T_done(w))
                    nc.scalar.copy(tail_T[:, :], q_bank[:, 0:128]).then_inc(tail_T_ready.sem, 1)
                else:
                    act.wait_ge(tail_1_done.sem, tail_1_done(w))
                    nc.scalar.activation(hidden_T[:, :], q_bank[:, 128:256], ACT.Relu,
                                         bias=fc1_bias_sb[:, 0:1]).then_inc(hidden_ready.sem, 1)

            def exponentials(u, q):
                if not exists(u):
                    return
                act.wait_ge(attended.sem, attended(u, q + 1))
                act.wait_ge(pv_done.sem, pv_done(*quad_before(u, q, 4)))
                nc.scalar.activation(probs[:, q, :], attend_bank[q % 2][:, :], ACT.Exp,
                                     scale=float(DK) ** -0.5).then_inc(exp_done.sem, 1)

            def evacuate_o(u):
                if not exists(u):
                    return
                act.wait_ge(pv_done.sem, pv_done(u))
                act.wait_ge(o_T_done.sem, o_T_done(plus(u, -1)))
                nc.scalar.copy(o_sb[:, :, :].rearrange("p q s -> p (q s)"), o_bank[:, :]).then_inc(o_ready.sem, 1)

            def evacuate_x_T(f):
                if not exists(f):
                    return
                act.wait_ge(x_T_done.sem, x_T_done(f))
                act.wait_ge(v_done.sem, v_done(plus(f, -1)))
                n = 1 if layer_of(f) == SELF else 2
                nc.scalar.copy(xc_T[:, 0:n, :].rearrange("p a s -> p (a s)"),
                               t_bank[:, 0:128 * n]).then_inc(xc_T_ready.sem, 1)

            def evacuate_negmax(u):
                if not exists(u):
                    return
                act.wait_ge(nm_T_done.sem, nm_T_done(u))
                before = plus(u, -1)
                act.wait_ge(negmax_done[slot_of(before)].sem, negmax_done[slot_of(before)](before))
                nc.scalar.copy(negmax_T[:, :], nm_T_ps).then_inc(negmax_T_ready.sem, 1)

            def high_parts(f, kind):
                if not exists(f):
                    return
                act.wait_ge((packed_k if kind else packed_q).sem, (packed_k if kind else packed_q)(plus(f, -1)))
                if layer_of(f) == OUTER:
                    act.wait_ge(biased_done.sem, biased_done(f, kind + 1))
                    src = biased[:, kind, :, :].rearrange("p q s -> p (q s)")
                else:
                    act.wait_ge((k_done if kind else q_done).sem, (k_done if kind else q_done)(f))
                    src = (k_bank if kind else q_bank)[:, :]
                nc.scalar.activation(low_hi[:, kind, :, :].rearrange("p q s -> p (q s)"), src, ACT.Copy,
                                     scale=low_rows[:, kind:kind + 1]).then_inc(
                                         (low_hi_k if kind else low_hi_q).sem, 1)

            def evacuate_v(f):
                if not exists(f):
                    return
                act.wait_ge(v_done.sem, v_done(f))
                nc.scalar.copy(v_aug[:, slot_of(f), :, 0:DK],
                               v_ps.rearrange("p (h k) -> p h k", k=DK)).then_inc(v_ready.sem, 1)

            def step(u):
                front, ahead = plus(u, AHEAD), plus(u, 1)
                tail_evac(plus(u, -1), 0)
                exponentials(u, 2)
                tail_evac(plus(u, -1), 1)
                exponentials(u, 3)
                evacuate_x_T(front)
                evacuate_o(u)
                evacuate_negmax(ahead)
                high_parts(front, 0)
                high_parts(front, 1)
                evacuate_v(front)
                exponentials(ahead, 0)
                exponentials(ahead, 1)

            act.wait_ge(bias_done, 2)
            act.wait_ge(rows_in, 16 * 3)
            act.wait_ge(pool_setup, N_POOL_SETUP)
            run_steps(act, step, -LOAD_AHEAD, UNITS + 1)

        @block.vector
        def _(dve):
            def prepare(f):
                if not exists(f) or layer_of(f) == OUTER:
                    return
                l, b = layer_of(f), slot_of(f)
                if l == SELF:
                    dve.wait_ge(x_loaded[b].sem, x_loaded[b](f))
                    src, mask = x_in, mask0
                else:
                    dve.wait_ge(x1_chain.sem, x1_chain(plus(f, -SLOTS)))
                    src, mask = x1, mask1
                nc.vector.tensor_scalar(junk[:, :], src[:, b, :], 0.0, 0.0, ALU.not_equal, ALU.add,
                                        accum_out=count[:, :]).then_inc(prep.sem, 1)
                dve.wait_ge(prep.sem, prep(f, 1))
                nc.vector.tensor_scalar(mask[:, b:b + 1], count[:, :], 0.0, None, ALU.is_gt).then_inc(prep.sem, 1)
                if l == CROSS:
                    dve.wait_ge(ctx_loaded[b].sem, ctx_loaded[b](f))
                    dve.wait_ge(x_T_done.sem, x_T_done(plus(f, -1)))
                    dve.wait_ge(prep.sem, prep(f, 2))
                    nc.vector.tensor_scalar(ctx_m[:, :], ctx[:, b, :], mask[:, b:b + 1], None,
                                            ALU.mult).then_inc(prep.sem, 1)

            def maxima(u, q):
                if not exists(u):
                    return
                dve.wait_ge(scored.sem, scored(u, q + 1))
                if q == 0:
                    dve.wait_ge(parts_chain.sem, parts_chain(plus(u, -1)))
                nc.vector.tensor_reduce(negmax[:, :].rearrange("p (j q) -> p j q", q=QUADS)[:, :, q],
                                        score_bank[q % 2][:, :].rearrange("p (j t) -> p j t", j=BLOCKS),
                                        AX_X, ALU.max, negate=True).then_inc(max_done.sem, 1)

            def split_maxima(u):
                if not exists(u):
                    return
                dve.wait_ge(max_done.sem, max_done(u))
                dve.wait_ge(nm_T_done.sem, nm_T_done(plus(u, -1)))
                nc.vector.tensor_copy(negmax_parts[:, 0, :], negmax[:, :]).then_inc(parts_chain.sem, 1)
                dve.wait_ge(parts_chain.sem, parts_chain(u, 1))
                nc.vector.tensor_tensor(negmax_parts[:, 1, :], negmax[:, :],
                                        negmax_parts[:, 0, :].bitcast(F32), ALU.subtract).then_inc(parts_chain.sem, 1)

            def add_bias(f, kind):
                if not exists(f) or layer_of(f) != OUTER:
                    return
                dve.wait_ge((k_done if kind else q_done).sem, (k_done if kind else q_done)(f))
                nc.vector.tensor_tensor(biased[:, kind, :, :],
                                        (k_bank if kind else q_bank)[:, :].rearrange("p (q s) -> p q s", q=QUADS),
                                        bias_col[:, 2 + kind, :].unsqueeze(2).broadcast_to([128, QUADS, S]),
                                        ALU.add).then_inc(biased_done.sem, 1)

            def split(f, kind):
                if not exists(f):
                    return
                b = slot_of(f)
                dve.wait_ge((low_hi_k if kind else low_hi_q).sem, (low_hi_k if kind else low_hi_q)(f))
                dst = packed[:, b, kind, :, :].rearrange("p q s -> p (q s)")
                hi = low_hi[:, kind, :, :].rearrange("p q s -> p (q s)").bitcast(F32)
                done = (packed_k if kind else packed_q).sem
                dve.wait_ge(attended.sem, attended(plus(f, -SLOTS)))
                if layer_of(f) == OUTER:
                    nc.vector.tensor_tensor(dst, biased[:, kind, :, :].rearrange("p q s -> p (q s)"), hi,
                                            ALU.subtract).then_inc(done, 1)
                else:
                    nc.vector.scalar_tensor_tensor(dst, (k_bank if kind else q_bank)[:, :],
                                                   bias_col[:, kind, 0:1], hi, ALU.add,
                                                   ALU.subtract).then_inc(done, 1)

            def spread_first(f):
                if not exists(f) or layer_of(f) == OUTER:
                    return
                dve.wait_ge(packed_q.sem, packed_q(f))
                dve.wait_ge(packed_k.sem, packed_k(f))
                dve.wait_ge(first_done.sem, first_done(plus(f, -1)))
                nc.vector.tensor_tensor(
                    first_q[:, :, 0:BLOCKS],
                    packed[:, slot_of(f), 0, :, 0:1].bitcast(F32).broadcast_to([128, QUADS, BLOCKS]),
                    block_mask[:, :].unsqueeze(1).broadcast_to([128, QUADS, BLOCKS]),
                    ALU.mult).then_inc(first_ready.sem, 1)

            def length_mask(f):
                if not exists(f) or layer_of(f) == OUTER:
                    return
                dve.wait_ge(first_done.sem, first_done(f))
                nc.vector.tensor_scalar(junk[:, :], k_bank[:, 0:S], 0.0, 0.0, ALU.not_equal, ALU.add,
                                        accum_out=length[:, :]).then_inc(len_chain.sem, 1)
                dve.wait_ge(len_chain.sem, len_chain(f, 1))
                nc.vector.reciprocal(len_inverse[:, :], length[:, :]).then_inc(len_chain.sem, 1)
                dve.wait_ge(len_chain.sem, len_chain(f, 2))
                nc.vector.tensor_scalar(len_big[:, :], length[:, :], len_inverse[:, :], -BIG, ALU.mult,
                                        ALU.mult).then_inc(len_chain.sem, 1)
                dve.wait_ge(len_chain.sem, len_chain(f, 3))
                before = plus(f, -1)
                dve.wait_ge(len_stored[slot_of(before)].sem, len_stored[slot_of(before)](before))
                nc.vector.tensor_scalar(len_mask[:, :], iota_t[:, :], length[:, :], len_big[:, :],
                                        ALU.is_ge, ALU.mult).then_inc(len_chain.sem, 1)

            def normalise(src, st, mv, ve, rs, ready, dst, chain, unit, at):
                dve.wait_ge(chain.sem, chain(unit, at))
                nc.vector.bn_stats(st[:, :], src[:, :]).then_inc(chain.sem, 1)
                dve.wait_ge(chain.sem, chain(unit, at + 1))
                nc.vector.memset(bubble[:, :], 0.0)
                nc.vector.bn_aggr(mv[:, :], st[:, :]).then_inc(chain.sem, 1)
                dve.wait_ge(chain.sem, chain(unit, at + 2))
                dve.wait_ge(ready.sem, ready(plus(unit, -1)))
                nc.vector.tensor_scalar(ve[:, :], mv[:, 1:2], EPS, None, ALU.add).then_inc(chain.sem, 1)
                dve.wait_ge(ready.sem, ready(unit))
                nc.vector.tensor_scalar(dst[:, :], src[:, :], mv[:, 0:1], rs[:, :], ALU.subtract,
                                        ALU.mult).then_inc(chain.sem, 1)

            def attention_out(u):
                if not exists(u):
                    return
                l, b = layer_of(u), slot_of(u)
                o_T = o_bank[:, :].rearrange("p (q j r) -> p j q r", q=QUADS, j=BLOCKS)
                dve.wait_ge(o_T_done.sem, o_T_done(u))
                dve.wait_ge(norm.sem, norm(plus(u, -1)))
                if layer_of(plus(u, -1)) == OUTER:
                    dve.wait_ge(ctx_v_ready.sem, ctx_v_ready(plus(u, -1)))
                nc.vector.reciprocal(recip[:, :].rearrange("p (j q) -> p j q", q=QUADS),
                                     o_T[:, :, :, DK]).then_inc(norm.sem, 1)
                dve.wait_ge(norm.sem, norm(u, 1))
                nc.vector.tensor_tensor(
                    z[:, :].rearrange("p (j q k) -> p j q k", j=BLOCKS, q=QUADS), o_T[:, :, :, 0:DK],
                    recip[:, :].rearrange("p (j q) -> p j q", q=QUADS).unsqueeze(3).broadcast_to(
                        [128, BLOCKS, QUADS, DK]), ALU.mult).then_inc(norm.sem, 1)
                if l == OUTER:
                    return
                dve.wait_ge(norm.sem, norm(u, 2))
                mask, res = (mask0, x_in) if l == SELF else (mask1, x1)
                nc.vector.scalar_tensor_tensor(y[:, :], z[:, :], mask[:, b:b + 1], res[:, b, :], ALU.mult,
                                               ALU.add).then_inc(norm.sem, 1)
                dve.wait_ge(x1_chain.sem, x1_chain(plus(u, -1)))
                dve.wait_ge(x2_chain.sem, x2_chain(plus(u, -1)))
                normalise(y, stats, mean_var, var_eps, rstd, rstd_ready, xn, norm, u, 3)

            def tail_out(w):
                if not exists(w) or layer_of(w) == SELF:
                    return
                l, b = layer_of(w), slot_of(w)
                if l == CROSS:
                    dve.wait_ge(x2_chain.sem, x2_chain(w))
                    nc.vector.scalar_tensor_tensor(tail_res[:, 0, :], rows_sb[:, FC2B, :], mask0[:, b:b + 1],
                                                   x2[:, b, :], ALU.mult, ALU.add).then_inc(tail_norm.sem, 1)
                    dve.wait_ge(tail_2_done.sem, tail_2_done(w))
                    dve.wait_ge(tail_norm.sem, tail_norm(w, 1))
                    nc.vector.scalar_tensor_tensor(y2[:, :], q_bank[:, 256:384], mask0[:, b:b + 1],
                                                   tail_res[:, 0, :], ALU.mult, ALU.add).then_inc(tail_norm.sem, 1)
                else:
                    dve.wait_ge(tail_1_done.sem, tail_1_done(w))
                    dve.wait_ge(outer_res_ready.sem, outer_res_ready(w))
                    nc.vector.tensor_tensor(y2[:, :], q_bank[:, 128:256], tail_res[:, 1, :],
                                            ALU.add).then_inc(tail_norm.sem, 1)
                last = plus(w, -1)
                if layer_of(last) == CROSS:
                    dve.wait_ge(x3_chain.sem, x3_chain(last))
                elif layer_of(last) == OUTER:
                    dve.wait_ge(y_chain.sem, y_chain(last))
                normalise(y2, stats2, mean_var2, var_eps2, rstd2, rstd2_ready, xn2, tail_norm, w,
                          2 if l == CROSS else 1)

            def step(u):
                front, ahead = plus(u, AHEAD), plus(u, 1)
                maxima(ahead, 0)
                prepare(front)
                maxima(ahead, 1)
                maxima(ahead, 2)
                tail_out(plus(u, -1))
                maxima(ahead, 3)
                split_maxima(ahead)
                attention_out(u)
                add_bias(front, 0)
                split(front, 0)
                add_bias(front, 1)
                split(front, 1)
                spread_first(front)
                length_mask(front)

            for b in range(2):
                nc.vector.memset(spread[:, b, :, :, :, :].rearrange("p a j q s -> p (a j q s)").bitcast(F32), 0.0).then_inc(zeroed[b], 1)
            nc.vector.memset(v_aug[:, :, :, :].rearrange("p b h r -> p (b h r)"), 0.0).then_inc(dve_setup, 1)
            dve.wait_ge(dve_setup, 1)
            nc.vector.memset(v_aug[:, :, :, DK:DK + 1].rearrange("p b h r -> p (b h) r"), 1.0).then_inc(dve_setup, 1)
            dve.wait_ge(weights_in, 16)
            dve.wait_ge(pool_zeros, 2)
            by_head = "p (j q k) -> p j q k"
            for l in range(LAYERS):
                for kind, ws in ((0, WQ), (1, WK)):
                    for term in range(TERMS):
                        for q in range(QUADS):
                            last = nc.vector.tensor_copy(
                                w_packed[:, 2 * l + kind, q, :, DK * term:DK * term + DK],
                                w_sb[:, ws[l], :].rearrange(by_head, j=BLOCKS, q=QUADS)[:, :, q, :])
            last.then_inc(dve_setup, 1)
            dve.wait_ge(rows_in, 16 * 3)
            for kind in range(2):
                for term in range(TERMS):
                    for q in range(QUADS):
                        last = nc.vector.tensor_copy(
                            bias_row[0:1, 2 + kind, q, :, DK * term:DK * term + DK],
                            qk_bias_sb[0:1, kind, :].rearrange(by_head, j=BLOCKS, q=QUADS)[:, :, q, :])
            last.then_inc(dve_setup, 1)
            dve.wait_ge(pool_setup, N_POOL_SETUP)
            nc.vector.tensor_copy(ident_r[:, :], ident[:, :]).then_inc(dve_setup, 1)
            nc.vector.tensor_copy(ident_b[:, :], ident[:, :]).then_inc(dve_setup, 1)
            dve.wait_ge(bias_ps, 1)
            nc.vector.tensor_copy(bias_col[:, :, :].rearrange("p a q -> p (a q)"),
                                  k_bank[:, 0:4 * QUADS]).then_inc(bias_done, 1)
            nc.vector.tensor_copy(low_rows[:, :], k_bank[:, 4 * QUADS:4 * QUADS + 2]).then_inc(bias_done, 1)
            dve.wait_ge(bias_done, 2)
            run_steps(dve, step, -LOAD_AHEAD, UNITS + 1)

        @block.gpsimd
        def _(pool):
            def affine(dst, gamma, beta, src, between, chain, unit, at, last_read):
                nc.gpsimd.tensor_tensor(between[:, :], src[:, :], rows_sb[:, gamma, :], ALU.mult).then_inc(chain.sem, 1)
                pool.wait_ge(chain.sem, chain(unit, 1))
                nc.gpsimd.tensor_tensor(dst, between[:, :], rows_sb[:, beta, :], ALU.add).then_inc(chain.sem, 1)

            def attention_norm(u):
                if not exists(u):
                    return
                l, b = layer_of(u), slot_of(u)
                if l != OUTER:
                    pool.wait_ge(norm.sem, norm(u, 6))
                    nc.gpsimd.tensor_tensor(rstd[:, :], var_eps[:, :], minus_half[:, :],
                                            ALU.pow).then_inc(rstd_ready.sem, 1)
                pool.wait_ge(norm.sem, norm(u))
                if l == SELF:
                    affine(x1[:, b, :], LN1G, LN1B, xn, scaled, x1_chain, u, 0, None)
                elif l == CROSS:
                    affine(x2[:, b, :], LN2G, LN2B, xn, scaled, x2_chain, u, 0, None)
                else:
                    pool.wait_ge(tail_T_done.sem, tail_T_done(plus(u, -1)))
                    nc.gpsimd.tensor_tensor(ctx_v[:, :], z[:, :], rows_sb[:, BV, :],
                                            ALU.add).then_inc(ctx_v_ready.sem, 1)
                    pool.wait_ge(tail_norm.sem, tail_norm(plus(u, -1)))
                    pool.wait_ge(x3_chain.sem, x3_chain(plus(u, -SLOTS)))
                    nc.gpsimd.tensor_tensor(tail_res[:, 1, :], x3[:, b, :], rows_sb[:, BO, :],
                                            ALU.add).then_inc(outer_res_ready.sem, 1)

            def tail_affine(w):
                if not exists(w) or layer_of(w) == SELF:
                    return
                b = slot_of(w)
                pool.wait_ge(tail_norm.sem, tail_norm(w, tail_norm.per[layer_of(w)] - 1))
                nc.gpsimd.tensor_tensor(rstd2[:, :], var_eps2[:, :], minus_half[:, :],
                                        ALU.pow).then_inc(rstd2_ready.sem, 1)
                pool.wait_ge(tail_norm.sem, tail_norm(w))
                if layer_of(w) == CROSS:
                    affine(x3[:, b, :], LN3G, LN3B, xn2, scaled2, x3_chain, w, 0, None)
                else:
                    affine(y_out[:, b % 2, :], GAMMA, BETA, xn2, scaled2, y_chain, w, 0, None)

            def settle(w):
                if exists(w) and layer_of(w) == OUTER:
                    pool.wait_ge(out_stored[slot_of(w)].sem, out_stored[slot_of(w)](w))

            def step(u):
                settle(plus(u, -3))
                tail_affine(plus(u, -1))
                attention_norm(u)

            nc.gpsimd.memset(w_packed[:, :, :, :, :].rearrange("p a q j r -> p (a q j r)"), 0.0).then_inc(pool_zeros, 1)
            nc.gpsimd.memset(bias_row[:, :, :, :, :].rearrange("p a q j r -> p (a q j r)"), 0.0).then_inc(pool_zeros, 1)
            nc.gpsimd.memset(ident[:, :], 0.0).then_inc(pool_zeros, 1)
            nc.gpsimd.memset(future_s[:, :], 0.0).then_inc(pool_zeros, 1)
            nc.gpsimd.memset(future_t[:, :], 0.0).then_inc(pool_zeros, 1)
            nc.gpsimd.memset(low_row[:, :, :, :].rearrange("p a j r -> p (a j r)"), 0.0).then_inc(pool_zeros, 1)
            nc.gpsimd.memset(block_mask[:, :], 0.0).then_inc(pool_zeros, 1)
            pool.wait_ge(pool_zeros, 7)
            setup = [0]

            def done(instruction):
                setup[0] += 1
                instruction.then_inc(pool_setup, 1)
                pool.wait_ge(pool_setup, setup[0])

            for kind in (0, 2):
                done(nc.gpsimd.memset(bias_row[0:1, kind, :, 0, SLEN_ROW:SLEN_ROW + 1], 1.0))
                done(nc.gpsimd.memset(bias_row[0:1, kind + 1, :, 0, NEGMAX_ROW:NEGMAX_ROW + 2], 1.0))
            done(nc.gpsimd.memset(low_row[0:1, 0, :, 2 * DK:3 * DK], 1.0))
            done(nc.gpsimd.memset(low_row[0:1, 1, :, DK:2 * DK], 1.0))
            done(nc.gpsimd.memset(one_sb[:, :], 1.0))
            done(nc.gpsimd.memset(minus_half[:, :], -0.5))
            for j in range(BLOCKS):
                done(nc.gpsimd.memset(block_mask[ROWS * j:ROWS * j + ROWS, j:j + 1], 1.0))
            done(nc.gpsimd.affine_select(out=ident[:, :], in_=ident[:, :], compare_op=ALU.not_equal, fill=1.0, base=0,
                                    pattern=[[-1, 128]], channel_multiplier=1))
            done(nc.gpsimd.affine_select(out=future_s[:, :], in_=future_s[:, :], compare_op=ALU.is_ge, fill=-BIG,
                                    base=0, pattern=[[-1, S]], channel_multiplier=1))
            done(nc.gpsimd.affine_select(out=future_t[:, :], in_=future_t[:, :], compare_op=ALU.is_ge, fill=-BIG,
                                    base=0, pattern=[[1, S]], channel_multiplier=-1))
            done(nc.gpsimd.iota(iota_t[:, :], pattern=[[1, S]], base=0, channel_multiplier=0,
                           allow_small_or_imprecise_dtypes=True))
            done(nc.gpsimd.memset(first_q[:, :, :].rearrange("p q r -> p (q r)"), 0.0))
            unused = first_q[:, :, BLOCKS:ROWS]
            done(nc.gpsimd.affine_select(out=unused, in_=unused, compare_op=ALU.not_equal, fill=1.0, base=-NEGMAX_ROW,
                                         pattern=[[0, QUADS], [0, ROWS - BLOCKS]], channel_multiplier=1))
            done(nc.gpsimd.memset(zero_rows[:, :].bitcast(F32), 0.0))
            for b in range(SLOTS):
                if b >= 2:
                    nc.gpsimd.memset(spread[:, b, :, :, :, :].rearrange("p a j q s -> p (a j q s)").bitcast(F32),
                                     0.0).then_inc(zeroed[b], 1)
                pool.wait_ge(zeroed[b], 1)
                view = spread[0:ROWS, b, 0, :, :, :].rearrange("p j q s -> p j (q s)")
                nc.gpsimd.affine_select(out=view, in_=view.bitcast(F32), compare_op=ALU.not_equal, fill=1.0, base=-TLEN_ROW,
                                        pattern=[[-1, BLOCKS], [0, QUADS * S]],
                                        channel_multiplier=1).then_inc(zeroed[b], 1)
            run_steps(pool, step, -LOAD_AHEAD, UNITS + 1)

        @block.sync
        def _(sp):
            def batch_of(unit):
                turn, n = unit
                number = n // PERIOD * SLOTS + n % SLOTS
                return number if turn is None else turn * SLOTS + number

            def load(v):
                if not exists(v) or layer_of(v) != SELF:
                    return
                b, n = slot_of(v), batch_of(v)
                at = slice(n, n + 1) if isinstance(n, int) else bass.ds(sp.snap(n), 1)
                sp.wait_ge(x_T_done.sem, x_T_done(plus(v, -SLOTS)))
                sp.dma_start(x_in[:, b, :], x[at, :, :].rearrange("o s d -> (o s) d")).then_inc(x_loaded[b].sem, 16)
                sp.dma_start(ctx[:, b, :], ctx_in[at, :, :].rearrange("o s d -> (o s) d")).then_inc(
                    ctx_loaded[b].sem, 16)

            def put_negmax(u):
                if not exists(u):
                    return
                b = slot_of(u)
                sp.wait_ge(negmax_T_ready.sem, negmax_T_ready(u))
                sp.dma_start(spread[NEGMAX_ROW:NEGMAX_ROW + 2, b, 0, :, :, :].rearrange("p j q s -> p (j q) s").bitcast(F32),
                             negmax_T[:, :].bitcast(F32)).then_inc(negmax_done[b].sem, 16)

            def put_spread(f):
                if not exists(f):
                    return
                b = slot_of(f)
                sp.wait_ge(packed_k.sem, packed_k(f))
                if f[0] is None and f[1] < SLOTS:
                    sp.wait_ge(zeroed[b], 2)
                for j in range(BLOCKS):
                    at = slice(ROWS * j, ROWS * j + DATA)
                    sp.dma_start(spread[at, b, :, j, :, :].bitcast(F32),
                                 packed[at, b, :, :, :].bitcast(F32)).then_inc(spread_done[b].sem, 16)

            def put_length(f):
                if not exists(f):
                    return
                b = slot_of(f)
                scored_row = spread[SLEN_ROW:SLEN_ROW + 1, b, 1, :, :, :].bitcast(F32)
                if layer_of(f) == OUTER:
                    sp.dma_start(scored_row.rearrange("p j q s -> p (j q) s"), zero_rows[:, :].bitcast(F32)).then_inc(
                        len_done[b].sem, 16)
                    return
                sp.wait_ge(len_chain.sem, len_chain(f))
                sp.dma_start(len_dram[b, :, :], len_mask[:, :].bitcast(F32)).then_inc(len_stored[b].sem, 16)
                sp.wait_ge(len_stored[b].sem, len_stored[b](f))
                by_head = len_dram[b, :, :].rearrange("(q r) s -> r q s", q=QUADS)[0:BLOCKS, :, :]
                sp.dma_start(scored_row, by_head.unsqueeze(0)).then_inc(len_done[b].sem, 16)
                sp.dma_start(packed[TLEN_ROW:TLEN_ROW + BLOCKS, b, 1, :, :].bitcast(F32), by_head).then_inc(len_done[b].sem, 16)

            def store(w):
                if not exists(w) or layer_of(w) != OUTER:
                    return
                b, n = slot_of(w), batch_of(w)
                dst = out[n:n + 1, :, :] if isinstance(n, int) else out[bass.ds(sp.snap(n), 1), :, :]
                sp.wait_ge(y_chain.sem, y_chain(w))
                sp.dma_start(dst.rearrange("o s d -> (o s) d"), y_out[:, b % 2, :]).then_inc(out_stored[b].sem, 16)

            def step(u):
                put_negmax(plus(u, 1))
                put_spread(plus(u, AHEAD))
                put_length(plus(u, AHEAD))
                load(plus(u, LOAD_AHEAD))
                store(plus(u, -1))

            sp.dma_start(w_sb[:, :, :], weights).then_inc(weights_in, 16)
            sp.dma_start(qk_bias_sb[:, :, :], qk_bias).then_inc(rows_in, 16)
            sp.dma_start(fc1_bias_sb[:, :], fc1_bias).then_inc(rows_in, 16)
            sp.dma_start(rows_sb[:, :, :], rows.unsqueeze(0).broadcast_to([128, N_ROWS, D])).then_inc(rows_in, 16)
            sp.wait_ge(pool_setup, N_POOL_SETUP)
            run_steps(sp, step, -LOAD_AHEAD, UNITS + 1)
            for b in range(SLOTS):
                sp.wait_ge(out_stored[b].sem, out_stored[b]((None, UNITS - 1)))
            for b in range(SLOTS):
                sp.wait_ge(len_stored[b].sem, len_stored[b]((None, UNITS - 1)))


def kernel(x, ctx_1024, L0_xattn_Wq1, L0_xattn_Wk1, L0_xattn_Wv1, L0_xattn_Wq2, L0_xattn_Wk2, L0_xattn_Wv2,
           L0_xattn_ln1_g, L0_xattn_ln1_b, L0_xattn_ln2_g, L0_xattn_ln2_b, L0_xattn_ln3_g, L0_xattn_ln3_b,
           L0_xattn_fc1_w, L0_xattn_fc1_b, L0_xattn_fc2_w, L0_xattn_fc2_b, L1_xattn_W_qkv, L1_xattn_b_qkv,
           L1_xattn_W_o, L1_xattn_b_o, L1_xattn_ln_gamma, L1_xattn_ln_beta):
    import numpy as np
    from concourse import bacc
    from concourse.bass_utils import run_bass_kernel_spmd

    def heads_last(w):
        return np.asarray(w).transpose(1, 0, 2).reshape(D, D)

    qkv = np.asarray(L1_xattn_W_qkv).reshape(3, D, D)
    qkv_bias = np.asarray(L1_xattn_b_qkv).reshape(3, D)
    weights = np.stack(
        [heads_last(w) for w in (L0_xattn_Wq1, L0_xattn_Wk1, L0_xattn_Wv1, L0_xattn_Wq2, L0_xattn_Wk2, L0_xattn_Wv2)]
        + [np.asarray(w).T for w in (qkv[0], qkv[1], qkv[2], L1_xattn_W_o, L0_xattn_fc1_w, L0_xattn_fc2_w)], axis=1)
    rows = np.stack([np.asarray(r) for r in (
        L0_xattn_ln1_g, L0_xattn_ln1_b, L0_xattn_ln2_g, L0_xattn_ln2_b, L0_xattn_ln3_g, L0_xattn_ln3_b,
        L0_xattn_fc2_b, L1_xattn_ln_gamma, L1_xattn_ln_beta, L1_xattn_b_o, qkv_bias[2])])
    arrays = {
        "x": np.asarray(x), "ctx": np.asarray(ctx_1024), "weights": np.ascontiguousarray(weights),
        "rows": rows, "qk_bias": np.ascontiguousarray(qkv_bias[0:2]).reshape(1, 2, D),
        "fc1_bias": np.asarray(L0_xattn_fc1_b).reshape(D, 1),
    }
    nc = bacc.Bacc("TRN2", target_bir_lowering=False, num_devices=1)
    ins = [nc.dram_tensor(f"{name}_dram", a.shape, mybir.dt.from_np(a.dtype), kind="ExternalInput").ap()
           for name, a in arrays.items()]
    out = nc.dram_tensor("out_dram", (B, S, D), F32, kind="ExternalOutput").ap()
    xattn_kernel(nc, *ins, out)
    got = run_bass_kernel_spmd(nc, [{f"{name}_dram": a for name, a in arrays.items()}], core_ids=[0])
    return got.results[0]["out_dram"]
```

```python
from contextlib import ExitStack

import concourse.bass as bass
from concourse import mybir

F32 = mybir.dt.float32
F32R = mybir.dt.float32r
BF16 = mybir.dt.bfloat16
ALU = mybir.AluOpType
ACT = mybir.ActivationFunctionType
AX_X = mybir.AxisListType.X

B, S, D, H = 16, 128, 128, 16
DK = D // H
BLOCKS = 4
QUADS = H // BLOCKS
ROWS = 128 // BLOCKS
TERMS = 3
DATA = TERMS * DK
NEGMAX_ROW, SLEN_ROW, TLEN_ROW = DATA, DATA + 2, DATA + 3
SELF, OUTER, CROSS = range(3)
LAYERS = 3
LAG = (0, 3, 1)
TO_CROSS = LAYERS * (LAG[CROSS] - LAG[SELF]) + CROSS - SELF
TO_OUTER = LAYERS * (LAG[OUTER] - LAG[CROSS]) + OUTER - CROSS
RING = 3
PERIOD = RING * LAYERS
STREAM = LAYERS * (B - 1 + LAG[OUTER]) + OUTER + 1
LOAD_AHEAD = 5
AHEAD = 3
LOOP_AT = 16
BIG = 1.0e30
EPS = 1e-5
WQ, WK, WV = ([0, 6, 3], [1, 7, 4], [2, 8, 5])
WO, FC1, FC2 = 9, 10, 11
N_WEIGHTS = 12
BIAS_PARTS = 3
LN1G, LN1B, LN2G, LN2B, LN3G, LN3B, FC2B, GAMMA, BETA, BO, BV = range(11)
N_ROWS = 11


def layer_of(unit):
    return unit[1] % LAYERS


def sequence_of(unit):
    return unit[1] // LAYERS - LAG[layer_of(unit)]


def ring_of(unit):
    return sequence_of(unit) % RING


def plus(unit, n):
    return unit[0], unit[1] + n


def exists(unit):
    return unit[0] is not None or 0 <= sequence_of(unit) < B


class Event:

    def __init__(self, sem, per, step=1, ring=None):
        self.sem, self.per, self.step, self.ring = sem, per, step, ring

    def __call__(self, unit, k=None):
        turn, n = unit
        count = 0
        for layer, per in self.per.items():
            sequences = (n - layer + LAYERS - 1) // LAYERS - LAG[layer]
            assert turn is None or sequences > 0
            sequences = min(max(sequences, 0), B)
            if self.ring is not None:
                sequences = (sequences - self.ring + RING - 1) // RING
            count += sequences * per
        if exists((None, n)) and self.ring in (None, ring_of(unit)):
            own = self.per.get(layer_of(unit), 0)
            count += own if k is None else min(k, own)
        if turn is None:
            return count * self.step
        assert count > 0
        a_turn = sum(self.per.values()) * (RING if self.ring is None else 1)
        return turn * (a_turn * self.step) + count * self.step


def run_steps(eng, step, first, last):
    turns = (LAYERS * B - LOAD_AHEAD - LOOP_AT) // PERIOD
    for n in range(first, LOOP_AT):
        step((None, n))
    with eng.Fori(0, turns) as turn:
        for n in range(LOOP_AT, LOOP_AT + PERIOD):
            step((turn, n))
    for n in range(LOOP_AT + turns * PERIOD, last):
        step((None, n))


def xattn_kernel(nc, x, ctx_in, weights, rows, qk_bias, fc1_bias, out):
    with ExitStack() as stack:
        def sb(name, shape, dt=F32):
            return stack.enter_context(nc.sbuf_tensor(name, shape, dt))

        def bank(name):
            return stack.enter_context(nc.psum_tensor(name, [128, 512], F32))

        def sem(name):
            return stack.enter_context(nc.semaphore(name))

        def event(name, per, step=1, ring=None):
            if isinstance(per, int):
                per = {l: per for l in range(LAYERS)}
            return Event(sem(name), per, step, ring)

        def ring_events(name, layer):
            return [event(f"{name}{r}", {layer: 1}, 16, r) for r in range(RING)]

        def layer_events(name, per):
            return {l: event(f"{name}{l}", {l: k}, 16) for l, k in per.items()}

        w_sb = sb("w_sb", [128, N_WEIGHTS, D])
        rows_sb = sb("rows_sb", [128, N_ROWS, D])
        qk_bias_sb = sb("qk_bias_sb", [1, 2, D])
        fc1_bias_sb = sb("fc1_bias_sb", [128, 1])
        w_packed = sb("w_packed", [128, 2 * LAYERS, QUADS, BLOCKS, ROWS])
        bias_row = sb("bias_row", [1, 2, QUADS, BLOCKS, ROWS])
        bias_rest = sb("bias_rest", [1, 2, 2 * QUADS * 128])
        bias_split = sb("bias_split", [1, BIAS_PARTS, 2, QUADS, 128], BF16)
        bias_parts = sb("bias_parts", [BIAS_PARTS, 2, QUADS, 128], BF16)
        ones_b = sb("ones_b", [BIAS_PARTS, S], BF16)
        one_sb = sb("one_sb", [1, 1])
        flag_row = sb("flag_row", [1, 4, BLOCKS, ROWS])
        flags = sb("flags", [128, 4])
        ident = sb("ident", [128, 128])
        ident_r = sb("ident_r", [128, 128], F32R)
        ident_b = sb("ident_b", [128, 128], BF16)
        future_s = sb("future_s", [128, 128], BF16)
        future_t = sb("future_t", [128, 128], BF16)
        iota_t = sb("iota_t", [H, S])
        block_mask = sb("block_mask", [128, BLOCKS])

        x_in = sb("x_in", [128, RING, D])
        ctx = sb("ctx", [128, RING, D])
        ctx_m = sb("ctx_m", [128, D])
        x1 = sb("x1", [128, RING, D])
        x2 = sb("x2", [128, RING, D])
        x3 = sb("x3", [128, RING, D])
        mask0 = sb("mask0", [128, RING])
        mask1 = sb("mask1", [128, RING])
        count = sb("count", [128, 1])
        junk = sb("junk", [128, 128])
        junk_2 = sb("junk_2", [H, S])
        xc_T = sb("xc_T", [128, 2, 128])
        q_sb = sb("q_sb", [128, QUADS, S])
        high_q = sb("high_q", [128, QUADS, S], F32R)
        high_k = sb("high_k", [128, QUADS, S], F32R)
        packed = sb("packed", [128, LAYERS, 2, QUADS, S], F32R)
        spread = sb("spread", [128, LAYERS, 2, BLOCKS, QUADS, S], F32R)
        first_q = sb("first_q", [128, QUADS * (H + 1)])
        length = sb("length", [H, 1])
        len_inverse = sb("len_inverse", [H, 1])
        len_big = sb("len_big", [H, 1])
        len_mask = sb("len_mask", [H, LAYERS, S], F32R)
        v_aug = sb("v_aug", [128, LAYERS, H, ROWS])
        negmax = sb("negmax", [128, H])
        negmax_parts = sb("negmax_parts", [128, 2, H], F32R)
        negmax_T = sb("negmax_T", [2 * H, S], F32R)
        probs = sb("probs", [128, 4, BLOCKS * S])
        o_sb = sb("o_sb", [128, QUADS, S])
        recip = sb("recip", [128, H])
        z = sb("z", [128, D])
        y = sb("y", [128, D])
        stats = sb("stats", [128, 6])
        mean_var = sb("mean_var", [128, 2])
        bubble = sb("bubble", [128, 1])
        var_eps = sb("var_eps", [128, 1])
        var_eps2 = sb("var_eps2", [128, 1])
        minus_half = sb("minus_half", [128, 1])
        rstd = sb("rstd", [128, 1])
        scaled = sb("scaled", [128, D])
        ctx_v = sb("ctx_v", [128, D])
        tail_res = sb("tail_res", [128, 2, D])
        tail_T = sb("tail_T", [128, 128])
        hidden_T = sb("hidden_T", [128, 128])
        y2 = sb("y2", [128, D])
        stats2 = sb("stats2", [128, 6])
        mean_var2 = sb("mean_var2", [128, 2])
        rstd2 = sb("rstd2", [128, 1])
        scaled2 = sb("scaled2", [128, D])
        y_out = sb("y_out", [128, RING, D])

        score_bank = [bank("score0"), bank("score1")]
        attend_bank = [bank("attend0"), bank("attend1")]
        o_bank = bank("o_bank")
        t_bank = bank("t_bank")
        q_bank = bank("q_bank")
        k_bank = bank("k_bank")
        x_T_ps, c_T_ps = t_bank[:, 0:128], t_bank[:, 128:256]
        v_ps = t_bank[:, 256:384]
        first_ps = k_bank[0:H, 0:S]
        tail_ps = [q_bank[:, 128 * part:128 * part + 128] for part in range(3)]
        nm_T_ps = attend_bank[0][0:2 * H, 0:128]

        weights_in = sem("weights_in")
        weights_in_2 = sem("weights_in_2")
        weights_packed = sem("weights_packed")
        rows_in = sem("rows_in")
        pool_setup = sem("pool_setup")
        pool_zeros = sem("pool_zeros")
        dve_setup = sem("dve_setup")
        zeroed = [sem(f"zeroed{l}") for l in range(LAYERS)]
        bias_ps = sem("bias_ps")
        bias_done = sem("bias_done")
        bias_chain = sem("bias_chain")
        bias_in = sem("bias_in")
        x_loaded = ring_events("x_loaded", SELF)
        ctx_loaded = ring_events("ctx_loaded", CROSS)
        out_stored = ring_events("out_stored", OUTER)
        spread_done = layer_events("spread_done", {SELF: BLOCKS, CROSS: BLOCKS, OUTER: BLOCKS})
        negmax_done = layer_events("negmax_done", {SELF: 1, CROSS: 1, OUTER: 1})
        len_done = layer_events("len_done", {SELF: 2, CROSS: 2})
        x_T_done = event("x_T_done", 1)
        q_done = event("q_done", 1)
        k_done = event("k_done", 1)
        v_done = event("v_done", 1)
        first_done = event("first_done", {SELF: 1, CROSS: 1})
        scored = event("scored", QUADS)
        nm_T_done = event("nm_T_done", 1)
        attended = event("attended", QUADS)
        pv_done = event("pv_done", QUADS)
        o_T_done = event("o_T_done", 1)
        tail_T_done = event("tail_T_done", {CROSS: 1, OUTER: 1})
        tail_1_done = event("tail_1_done", {CROSS: 1, OUTER: 1})
        tail_2_done = event("tail_2_done", {CROSS: 1})
        xc_T_ready = event("xc_T_ready", 1)
        high_q_ready = event("high_q_ready", 1)
        high_k_ready = event("high_k_ready", 1)
        q_sb_ready = event("q_sb_ready", 1)
        v_ready = event("v_ready", 1)
        negmax_T_ready = event("negmax_T_ready", 1)
        exp_done = event("exp_done", QUADS)
        o_ready = event("o_ready", 1)
        tail_T_ready = event("tail_T_ready", {CROSS: 1, OUTER: 1})
        hidden_ready = event("hidden_ready", {CROSS: 1})
        prep = event("prep", {SELF: 2, CROSS: 3})
        packed_k = event("packed_k", 1)
        len_chain = event("len_chain", {SELF: 4, CROSS: 4})
        max_done = event("max_done", QUADS)
        parts_chain = event("parts_chain", 2)
        norm = event("norm", {SELF: 7, CROSS: 7, OUTER: 2})
        tail_norm = event("tail_norm", {CROSS: 6, OUTER: 5})
        x1_ready = event("x1_ready", {SELF: 1})
        x2_ready = event("x2_ready", {CROSS: 1})
        x3_ready = event("x3_ready", {CROSS: 1})
        y_ready = event("y_ready", {OUTER: 1})
        rstd_ready = event("rstd_ready", {SELF: 1, CROSS: 1})
        rstd2_ready = event("rstd2_ready", {CROSS: 1, OUTER: 1})
        packed_q = event("packed_q", 1)
        first_ready = event("first_ready", {SELF: 1, CROSS: 1})
        outer_ctx_ready = event("outer_ctx_ready", {OUTER: 1})
        outer_res_ready = event("outer_res_ready", {OUTER: 1})

        block = stack.enter_context(nc.Block())

        def quad_before(unit, q, n):
            return plus(unit, (q - n) // QUADS), (q - n) % QUADS + 1

        def tail_raises(w):
            return tail_norm(w, 2 if layer_of(w) == CROSS else 1)

        N_POOL_SETUP, N_DVE_SETUP = 18, 4

        @block.tensor
        def _(pe):
            def front_transpose(f):
                if not exists(f):
                    return
                l, r = layer_of(f), ring_of(f)
                pe.wait_ge(v_ready.sem, v_ready(plus(f, -1)))
                if l == SELF:
                    pe.wait_ge(x_loaded[r].sem, x_loaded[r](f))
                    nc.tensor.transpose(x_T_ps, x_in[:, r, :], ident[:, :]).then_inc(x_T_done.sem, 1)
                elif l == CROSS:
                    pe.wait_ge(x1_ready.sem, x1_ready(plus(f, -TO_CROSS)))
                    pe.wait_ge(prep.sem, prep(f))
                    nc.tensor.transpose(c_T_ps, ctx_m[:, :], ident[:, :])
                    nc.tensor.transpose(x_T_ps, x1[:, r, :], ident[:, :]).then_inc(x_T_done.sem, 1)
                else:
                    pe.wait_ge(ctx_loaded[r].sem, ctx_loaded[r](plus(f, -TO_OUTER)))
                    nc.tensor.transpose(c_T_ps, ctx[:, r, :], ident[:, :])
                    pe.wait_ge(x3_ready.sem, x3_ready(plus(f, -TO_OUTER)))
                    nc.tensor.transpose(x_T_ps, x3[:, r, :], ident[:, :]).then_inc(x_T_done.sem, 1)

            def project(f, kind):
                if not exists(f):
                    return
                l = layer_of(f)
                pe.wait_ge(xc_T_ready.sem, xc_T_ready(f))
                if f[0] is None:
                    pe.wait_ge(weights_packed, 2)
                if f[0] is None and l == OUTER:
                    pe.wait_ge(bias_in, 16)
                if kind == 0:
                    pe.wait_ge(high_q_ready.sem, high_q_ready(plus(f, -1)))
                    pe.wait_ge(tail_norm.sem, tail_raises(plus(f, -AHEAD - 1)))
                else:
                    pe.wait_ge(packed_k.sem, packed_k(plus(f, -1)))
                    pe.wait_ge(len_chain.sem, len_chain(plus(f, -1), 1))
                src = xc_T[:, 1 if kind and l != SELF else 0, :]
                dst = k_bank if kind else q_bank
                for q in range(QUADS):
                    last = nc.tensor.matmul(dst[:, q * S:(q + 1) * S], w_packed[:, 2 * l + kind, q, :, :],
                                            src, start=True, stop=l != OUTER)
                    if l == OUTER:
                        last = nc.tensor.matmul(dst[:, q * S:(q + 1) * S], bias_parts[:, kind, q, :],
                                                ones_b[:, :], start=False, stop=True)
                last.then_inc((k_done if kind else q_done).sem, 1)

            def project_v(f):
                if not exists(f):
                    return
                l = layer_of(f)
                nc.tensor.matmul(v_ps, xc_T[:, 0 if l == SELF else 1, :], w_sb[:, WV[l], :],
                                 start=True, stop=True).then_inc(v_done.sem, 1)

            def first_scores(f):
                if not exists(f) or layer_of(f) == OUTER:
                    return
                pe.wait_ge(first_ready.sem, first_ready(f))
                pe.wait_ge(packed_k.sem, packed_k(f))
                for q in range(QUADS):
                    last = nc.tensor.matmul(first_ps, first_q[:, H * q:H * q + H],
                                            packed[:, layer_of(f), 1, q, :].bitcast(F32),
                                            start=q == 0, stop=q == QUADS - 1)
                last.then_inc(first_done.sem, 1)

            def score(u, q):
                if not exists(u):
                    return
                l = layer_of(u)
                if q == 0:
                    pe.wait_ge(spread_done[l].sem, spread_done[l](u))
                    if l != OUTER:
                        pe.wait_ge(len_done[l].sem, len_done[l](u))
                pe.wait_ge(max_done.sem, max_done(*quad_before(u, q, 2)))
                dst = score_bank[q % 2]
                last = nc.tensor.matmul(dst[:, :], packed[:, l, 0, q, :], spread[:, l, 1, :, q, :],
                                        start=True, stop=l != SELF)
                if l == SELF:
                    last = nc.tensor.matmul(dst[:, :], ident_b[:, :],
                                            future_s[:, :].unsqueeze(1).broadcast_to([128, BLOCKS, S]),
                                            start=False, stop=True)
                last.then_inc(scored.sem, 1)

            def transpose_negmax(u):
                if not exists(u):
                    return
                pe.wait_ge(parts_chain.sem, parts_chain(u))
                pe.wait_ge(exp_done.sem, exp_done(plus(u, -1)))
                nc.tensor.transpose(nm_T_ps.bitcast(F32R), negmax_parts[:, :, :].rearrange("p a h -> p (a h)"),
                                    ident_r[:, :]).then_inc(nm_T_done.sem, 1)

            def attend(u, q):
                if not exists(u):
                    return
                l = layer_of(u)
                if q == 0:
                    pe.wait_ge(negmax_done[l].sem, negmax_done[l](u))
                pe.wait_ge(exp_done.sem, exp_done(*quad_before(u, q, 2)))
                dst = attend_bank[q % 2]
                last = nc.tensor.matmul(dst[:, :], packed[:, l, 1, q, :], spread[:, l, 0, :, q, :],
                                        start=True, stop=l != SELF)
                if l == SELF:
                    last = nc.tensor.matmul(dst[:, :], ident_b[:, :],
                                            future_t[:, :].unsqueeze(1).broadcast_to([128, BLOCKS, S]),
                                            start=False, stop=True)
                last.then_inc(attended.sem, 1)

            def values(u):
                if not exists(u):
                    return
                pe.wait_ge(v_ready.sem, v_ready(u))
                pe.wait_ge(norm.sem, norm(plus(u, -1), 2))
                for q in range(QUADS):
                    pe.wait_ge(exp_done.sem, exp_done(u, q + 1))
                    for j in range(BLOCKS):
                        last = nc.tensor.matmul(o_bank[32 * j:32 * j + 32, q * S:(q + 1) * S],
                                                v_aug[:, layer_of(u), BLOCKS * j + q, :],
                                                probs[:, q, j * S:(j + 1) * S], start=True, stop=True)
                    last.then_inc(pv_done.sem, 1)

            def transpose_o(u):
                if not exists(u):
                    return
                pe.wait_ge(o_ready.sem, o_ready(u))
                for q in range(QUADS):
                    last = nc.tensor.transpose(o_bank[:, q * S:(q + 1) * S], o_sb[:, q, :], ident[:, :])
                last.then_inc(o_T_done.sem, 1)

            def tail(w, part):
                if not exists(w) or layer_of(w) == SELF or (part == 2 and layer_of(w) == OUTER):
                    return
                l, r = layer_of(w), ring_of(w)
                if part == 0:
                    pe.wait_ge(high_q_ready.sem, high_q_ready(plus(w, AHEAD)))
                    if l == CROSS:
                        pe.wait_ge(x2_ready.sem, x2_ready(w))
                    else:
                        pe.wait_ge(outer_ctx_ready.sem, outer_ctx_ready(w))
                    nc.tensor.transpose(tail_ps[0], x2[:, r, :] if l == CROSS else ctx_v[:, :],
                                        ident[:, :]).then_inc(tail_T_done.sem, 1)
                elif part == 1:
                    pe.wait_ge(tail_T_ready.sem, tail_T_ready(w))
                    if l == CROSS:
                        mm = nc.tensor.matmul(tail_ps[1], w_sb[:, FC1, :], tail_T[:, :],
                                              start=True, stop=True)
                    else:
                        mm = nc.tensor.matmul(tail_ps[1], tail_T[:, :], w_sb[:, WO, :],
                                              start=True, stop=True)
                    mm.then_inc(tail_1_done.sem, 1)
                else:
                    pe.wait_ge(hidden_ready.sem, hidden_ready(w))
                    nc.tensor.matmul(tail_ps[2], hidden_T[:, :], w_sb[:, FC2, :],
                                     start=True, stop=True).then_inc(tail_2_done.sem, 1)

            def step(u):
                before, last_front, front, ahead = plus(u, -1), plus(u, AHEAD - 1), plus(u, AHEAD), plus(u, 1)
                attend(u, 0)
                score(ahead, 0)
                attend(u, 1)
                score(ahead, 1)
                attend(u, 2)
                score(ahead, 2)
                attend(u, 3)
                score(ahead, 3)
                front_transpose(front)
                tail(before, 0)
                first_scores(last_front)
                values(u)
                transpose_negmax(ahead)
                tail(before, 1)
                project(front, 1)
                tail(before, 2)
                transpose_o(u)
                project_v(front)
                project(front, 0)

            pe.wait_ge(weights_in, 16)
            pe.wait_ge(pool_setup, N_POOL_SETUP)
            pe.wait_ge(dve_setup, N_DVE_SETUP)
            for kind in range(4):
                last = nc.tensor.matmul(k_bank[:, kind:kind + 1], flag_row[0:1, kind, :, :], one_sb[:, :],
                                        start=True, stop=True)
            last.then_inc(bias_ps, 1)
            pe.wait_ge(bias_done, 1)
            run_steps(pe, step, -LOAD_AHEAD, STREAM + 2)

        @block.scalar
        def _(act):
            def tail_evac(w, part):
                if not exists(w) or layer_of(w) == SELF or (part == 1 and layer_of(w) == OUTER):
                    return
                if part == 0:
                    act.wait_ge(tail_T_done.sem, tail_T_done(w))
                    nc.scalar.copy(tail_T[:, :], tail_ps[0]).then_inc(tail_T_ready.sem, 1)
                else:
                    act.wait_ge(tail_1_done.sem, tail_1_done(w))
                    nc.scalar.activation(hidden_T[:, :], tail_ps[1], ACT.Relu,
                                         bias=fc1_bias_sb[:, 0:1]).then_inc(hidden_ready.sem, 1)

            def exponentials(u, q):
                if not exists(u):
                    return
                act.wait_ge(attended.sem, attended(u, q + 1))
                act.wait_ge(pv_done.sem, pv_done(*quad_before(u, q, 4)))
                nc.scalar.activation(probs[:, q, :], attend_bank[q % 2][:, :], ACT.Exp,
                                     scale=float(DK) ** -0.5).then_inc(exp_done.sem, 1)

            def evacuate_o(u):
                if not exists(u):
                    return
                act.wait_ge(pv_done.sem, pv_done(u))
                act.wait_ge(o_T_done.sem, o_T_done(plus(u, -1)))
                nc.scalar.copy(o_sb[:, :, :].rearrange("p q s -> p (q s)"), o_bank[:, :]).then_inc(o_ready.sem, 1)

            def evacuate_x_T(f):
                if not exists(f):
                    return
                act.wait_ge(x_T_done.sem, x_T_done(f))
                act.wait_ge(q_done.sem, q_done(plus(f, -1)))
                n = 1 if layer_of(f) == SELF else 2
                nc.scalar.copy(xc_T[:, 0:n, :].rearrange("p a s -> p (a s)"),
                               t_bank[:, 0:128 * n]).then_inc(xc_T_ready.sem, 1)

            def evacuate_negmax(u):
                if not exists(u):
                    return
                act.wait_ge(nm_T_done.sem, nm_T_done(u))
                before = plus(u, -1)
                last = negmax_done[layer_of(before)]
                act.wait_ge(last.sem, last(before))
                nc.scalar.copy(negmax_T[:, :], nm_T_ps).then_inc(negmax_T_ready.sem, 1)

            def high_k_parts(f):
                if not exists(f):
                    return
                act.wait_ge(packed_k.sem, packed_k(plus(f, -1)))
                act.wait_ge(k_done.sem, k_done(f))
                nc.scalar.activation(high_k[:, :, :].rearrange("p q s -> p (q s)"), k_bank[:, :], ACT.Copy,
                                     scale=flags[:, 1:2]).then_inc(high_k_ready.sem, 1)

            def evacuate_q(f):
                if not exists(f):
                    return
                act.wait_ge(q_done.sem, q_done(f))
                act.wait_ge(packed_q.sem, packed_q(plus(f, -1)))
                dst = q_sb[:, :, :].rearrange("p q s -> p (q s)")
                if layer_of(f) == OUTER:
                    nc.scalar.copy(dst, q_bank[:, :]).then_inc(q_sb_ready.sem, 1)
                else:
                    nc.scalar.activation(dst, q_bank[:, :], ACT.Identity,
                                         bias=flags[:, 2:3]).then_inc(q_sb_ready.sem, 1)

            def high_q_parts(f):
                if not exists(f):
                    return
                nc.scalar.activation(high_q[:, :, :].rearrange("p q s -> p (q s)"), q_bank[:, :], ACT.Copy,
                                     scale=flags[:, 0:1]).then_inc(high_q_ready.sem, 1)

            def evacuate_v(f):
                if not exists(f):
                    return
                act.wait_ge(v_done.sem, v_done(f))
                nc.scalar.copy(v_aug[:, layer_of(f), :, 0:DK],
                               v_ps.rearrange("p (h k) -> p h k", k=DK)).then_inc(v_ready.sem, 1)

            def step(u):
                front = plus(u, AHEAD)
                exponentials(u, 0)
                exponentials(u, 1)
                exponentials(u, 2)
                exponentials(u, 3)
                evacuate_x_T(front)
                tail_evac(plus(u, -1), 0)
                evacuate_negmax(plus(u, 1))
                tail_evac(plus(u, -1), 1)
                evacuate_o(u)
                evacuate_v(front)
                high_k_parts(front)
                evacuate_q(front)
                high_q_parts(front)

            act.wait_ge(weights_in_2, 16)
            act.wait_ge(pool_zeros, 1)
            for l in (CROSS, OUTER):
                for kind, ws in ((0, WQ), (1, WK)):
                    for term in range(TERMS):
                        last = nc.scalar.copy(
                            w_packed[:, 2 * l + kind, :, :, DK * term:DK * term + DK],
                            w_sb[:, ws[l], :].rearrange("p (j q k) -> p q j k", j=BLOCKS, q=QUADS))
            last.then_inc(weights_packed, 1)
            act.wait_ge(bias_done, 1)
            act.wait_ge(rows_in, 16 * 3)
            act.wait_ge(pool_setup, N_POOL_SETUP)
            run_steps(act, step, -LOAD_AHEAD, STREAM + 2)

        @block.vector
        def _(dve):
            def prepare(f, layer, part):
                if not exists(f) or layer_of(f) != layer:
                    return
                l, r = layer_of(f), ring_of(f)
                src, mask = (x_in, mask0) if l == SELF else (x1, mask1)
                if part == 0:
                    dve.wait_ge(prep.sem, prep(plus(f, -1)))
                    if l == SELF:
                        dve.wait_ge(x_loaded[r].sem, x_loaded[r](f))
                    else:
                        dve.wait_ge(x1_ready.sem, x1_ready(plus(f, -TO_CROSS)))
                    nc.vector.tensor_scalar(junk[:, :], src[:, r, :], 0.0, 0.0, ALU.not_equal, ALU.add,
                                            accum_out=count[:, :]).then_inc(prep.sem, 1)
                elif part == 1:
                    dve.wait_ge(prep.sem, prep(f, 1))
                    nc.vector.tensor_scalar(mask[:, r:r + 1], count[:, :], 0.0, None, ALU.is_gt).then_inc(prep.sem, 1)
                else:
                    dve.wait_ge(ctx_loaded[r].sem, ctx_loaded[r](f))
                    dve.wait_ge(x_T_done.sem, x_T_done(plus(f, -LAYERS)))
                    dve.wait_ge(prep.sem, prep(f, 2))
                    nc.vector.tensor_scalar(ctx_m[:, :], ctx[:, r, :], mask[:, r:r + 1], None,
                                            ALU.mult).then_inc(prep.sem, 1)

            def maxima(u, q):
                if not exists(u):
                    return
                dve.wait_ge(scored.sem, scored(u, q + 1))
                if q == 0:
                    dve.wait_ge(parts_chain.sem, parts_chain(plus(u, -1)))
                nc.vector.tensor_reduce(negmax[:, :].rearrange("p (j q) -> p j q", q=QUADS)[:, :, q],
                                        score_bank[q % 2][:, :].rearrange("p (j t) -> p j t", j=BLOCKS),
                                        AX_X, ALU.max, negate=True).then_inc(max_done.sem, 1)

            def split_maxima(u, part):
                if not exists(u):
                    return
                if part == 0:
                    dve.wait_ge(max_done.sem, max_done(u))
                    dve.wait_ge(nm_T_done.sem, nm_T_done(plus(u, -1)))
                    nc.vector.tensor_copy(negmax_parts[:, 0, :], negmax[:, :]).then_inc(parts_chain.sem, 1)
                else:
                    dve.wait_ge(parts_chain.sem, parts_chain(u, 1))
                    nc.vector.tensor_tensor(negmax_parts[:, 1, :], negmax[:, :],
                                            negmax_parts[:, 0, :].bitcast(F32), ALU.subtract).then_inc(parts_chain.sem, 1)

            def split_k(f):
                if not exists(f):
                    return
                l = layer_of(f)
                dve.wait_ge(high_k_ready.sem, high_k_ready(f))
                dst = packed[:, l, 1, :, :].rearrange("p q s -> p (q s)")
                high = high_k[:, :, :].rearrange("p q s -> p (q s)").bitcast(F32)
                dve.wait_ge(attended.sem, attended(plus(f, -LAYERS)))
                if l == OUTER:
                    nc.vector.tensor_tensor(dst, k_bank[:, :], high, ALU.subtract).then_inc(packed_k.sem, 1)
                else:
                    nc.vector.scalar_tensor_tensor(dst, k_bank[:, :], flags[:, 3:4], high, ALU.add,
                                                   ALU.subtract).then_inc(packed_k.sem, 1)

            def length_mask(f, part):
                if not exists(f) or layer_of(f) == OUTER:
                    return
                l = layer_of(f)
                if part == 0:
                    dve.wait_ge(first_done.sem, first_done(f))
                    nc.vector.tensor_scalar(junk_2[:, :], first_ps, 0.0, 0.0, ALU.not_equal, ALU.add,
                                            accum_out=length[:, :]).then_inc(len_chain.sem, 1)
                elif part == 1:
                    dve.wait_ge(len_chain.sem, len_chain(f, 1))
                    nc.vector.reciprocal(len_inverse[:, :], length[:, :]).then_inc(len_chain.sem, 1)
                elif part == 2:
                    dve.wait_ge(len_chain.sem, len_chain(f, 2))
                    nc.vector.tensor_scalar(len_big[:, :], length[:, :], len_inverse[:, :], -BIG, ALU.mult,
                                            ALU.mult).then_inc(len_chain.sem, 1)
                else:
                    dve.wait_ge(len_chain.sem, len_chain(f, 3))
                    before = plus(f, -LAYERS)
                    dve.wait_ge(len_done[l].sem, len_done[l](before))
                    nc.vector.tensor_scalar(len_mask[:, l, :], iota_t[:, :], length[:, :], len_big[:, :],
                                            ALU.is_ge, ALU.mult).then_inc(len_chain.sem, 1)

            def bn_stats(st, src, chain, unit, at):
                dve.wait_ge(chain.sem, chain(unit, at))
                nc.vector.bn_stats(st[:, :], src[:, :]).then_inc(chain.sem, 1)

            def bn_aggregate(mv, st, chain, unit, at):
                dve.wait_ge(chain.sem, chain(unit, at))
                nc.vector.memset(bubble[:, :], 0.0)
                nc.vector.bn_aggr(mv[:, :], st[:, :]).then_inc(chain.sem, 1)

            def add_eps(ve, mv, ready, chain, unit, at):
                dve.wait_ge(chain.sem, chain(unit, at))
                dve.wait_ge(ready.sem, ready(plus(unit, -1)))
                nc.vector.tensor_scalar(ve[:, :], mv[:, 1:2], EPS, None, ALU.add).then_inc(chain.sem, 1)

            def centre(dst, src, mv, gamma, chain):
                nc.vector.scalar_tensor_tensor(dst[:, :], src[:, :], mv[:, 0:1], rows_sb[:, gamma, :], ALU.subtract,
                                               ALU.mult).then_inc(chain.sem, 1)

            def finish(dst, centred, rs, beta, done):
                nc.vector.scalar_tensor_tensor(dst, centred[:, :], rs[:, 0:1], rows_sb[:, beta, :], ALU.mult,
                                               ALU.add).then_inc(done.sem, 1)

            def attention_out(u, part):
                if not exists(u) or (layer_of(u) == OUTER and part >= 2):
                    return
                l, r = layer_of(u), ring_of(u)
                o_T = o_bank[:, :].rearrange("p (q j r) -> p j q r", q=QUADS, j=BLOCKS)
                if part == 0:
                    dve.wait_ge(o_T_done.sem, o_T_done(u))
                    nc.vector.reciprocal(recip[:, :].rearrange("p (j q) -> p j q", q=QUADS),
                                         o_T[:, :, :, DK]).then_inc(norm.sem, 1)
                elif part == 1:
                    dve.wait_ge(norm.sem, norm(u, 1))
                    dve.wait_ge(outer_ctx_ready.sem, outer_ctx_ready(plus(u, -1)))
                    nc.vector.tensor_tensor(
                        z[:, :].rearrange("p (j q k) -> p j q k", j=BLOCKS, q=QUADS), o_T[:, :, :, 0:DK],
                        recip[:, :].rearrange("p (j q) -> p j q", q=QUADS).unsqueeze(3).broadcast_to(
                            [128, BLOCKS, QUADS, DK]), ALU.mult).then_inc(norm.sem, 1)
                elif part == 2:
                    dve.wait_ge(norm.sem, norm(u, 2))
                    mask, res = (mask0, x_in) if l == SELF else (mask1, x1)
                    nc.vector.scalar_tensor_tensor(y[:, :], z[:, :], mask[:, r:r + 1], res[:, r, :], ALU.mult,
                                                   ALU.add).then_inc(norm.sem, 1)
                elif part == 3:
                    bn_stats(stats, y, norm, u, 3)
                elif part == 4:
                    bn_aggregate(mean_var, stats, norm, u, 4)
                elif part == 5:
                    add_eps(var_eps, mean_var, rstd_ready, norm, u, 5)
                elif part == 6:
                    dve.wait_ge(x1_ready.sem, x1_ready(plus(u, -1)))
                    dve.wait_ge(x2_ready.sem, x2_ready(plus(u, -1)))
                    centre(scaled, y, mean_var, LN1G if l == SELF else LN2G, norm)
                else:
                    dve.wait_ge(norm.sem, norm(u))
                    dve.wait_ge(rstd_ready.sem, rstd_ready(u))
                    if l == SELF:
                        finish(x1[:, r, :], scaled, rstd, LN1B, x1_ready)
                    else:
                        finish(x2[:, r, :], scaled, rstd, LN2B, x2_ready)

            def tail_out(w, part):
                if not exists(w) or layer_of(w) == SELF or (layer_of(w) == OUTER and part == 0):
                    return
                l, r = layer_of(w), ring_of(w)
                at = 2 if l == CROSS else 1
                if part == 0:
                    dve.wait_ge(x2_ready.sem, x2_ready(w))
                    nc.vector.scalar_tensor_tensor(tail_res[:, 0, :], rows_sb[:, FC2B, :], mask0[:, r:r + 1],
                                                   x2[:, r, :], ALU.mult, ALU.add).then_inc(tail_norm.sem, 1)
                elif part == 1 and l == CROSS:
                    dve.wait_ge(tail_2_done.sem, tail_2_done(w))
                    dve.wait_ge(tail_norm.sem, tail_norm(w, 1))
                    nc.vector.scalar_tensor_tensor(y2[:, :], tail_ps[2], mask0[:, r:r + 1],
                                                   tail_res[:, 0, :], ALU.mult, ALU.add).then_inc(tail_norm.sem, 1)
                elif part == 1:
                    dve.wait_ge(tail_1_done.sem, tail_1_done(w))
                    dve.wait_ge(outer_res_ready.sem, outer_res_ready(w))
                    nc.vector.tensor_tensor(y2[:, :], tail_ps[1], tail_res[:, 1, :],
                                            ALU.add).then_inc(tail_norm.sem, 1)
                elif part == 2:
                    bn_stats(stats2, y2, tail_norm, w, at)
                elif part == 3:
                    bn_aggregate(mean_var2, stats2, tail_norm, w, at + 1)
                elif part == 4:
                    add_eps(var_eps2, mean_var2, rstd2_ready, tail_norm, w, at + 2)
                elif part == 5:
                    dve.wait_ge(x3_ready.sem, x3_ready(plus(w, -1)))
                    dve.wait_ge(y_ready.sem, y_ready(plus(w, -1)))
                    centre(scaled2, y2, mean_var2, LN3G if l == CROSS else GAMMA, tail_norm)
                else:
                    dve.wait_ge(tail_norm.sem, tail_norm(w))
                    dve.wait_ge(rstd2_ready.sem, rstd2_ready(w))
                    if l == CROSS:
                        finish(x3[:, r, :], scaled2, rstd2, LN3B, x3_ready)
                        return
                    last = plus(w, -LAYERS)
                    if exists(last):
                        stored = out_stored[ring_of(last)]
                        dve.wait_ge(stored.sem, stored(last))
                    finish(y_out[:, r, :], scaled2, rstd2, BETA, y_ready)

            def step(u):
                before, last_front, front = plus(u, -1), plus(u, AHEAD - 1), plus(u, AHEAD)
                ahead, next_front = plus(u, 1), plus(u, AHEAD + 1)
                maxima(ahead, 0)
                attention_out(before, 6)
                maxima(ahead, 1)
                attention_out(before, 7)
                tail_out(plus(u, -2), 6)
                maxima(ahead, 2)
                maxima(ahead, 3)
                split_maxima(ahead, 0)
                length_mask(last_front, 0)
                split_maxima(ahead, 1)
                length_mask(last_front, 1)
                length_mask(last_front, 2)
                tail_out(before, 0)
                length_mask(last_front, 3)
                prepare(last_front, SELF, 0)
                tail_out(before, 1)
                prepare(last_front, SELF, 1)
                prepare(next_front, CROSS, 0)
                prepare(next_front, CROSS, 1)
                prepare(next_front, CROSS, 2)
                attention_out(u, 0)
                tail_out(before, 2)
                attention_out(u, 1)
                tail_out(before, 3)
                attention_out(u, 2)
                tail_out(before, 4)
                attention_out(u, 3)
                split_k(front)
                tail_out(before, 5)
                attention_out(u, 4)
                attention_out(u, 5)

            nc.vector.memset(spread[:, SELF, :, :, :, :].rearrange("p a j q s -> p (a j q s)").bitcast(F32),
                             0.0).then_inc(zeroed[SELF], 1)
            nc.vector.memset(v_aug[:, :, :, :].rearrange("p b h r -> p (b h r)"), 0.0).then_inc(dve_setup, 1)
            dve.wait_ge(dve_setup, 1)
            nc.vector.memset(v_aug[:, :, :, DK:DK + 1].rearrange("p b h r -> p (b h) r"), 1.0).then_inc(dve_setup, 1)
            dve.wait_ge(weights_in, 16)
            dve.wait_ge(pool_zeros, 2)
            for kind, ws in ((0, WQ), (1, WK)):
                for term in range(TERMS):
                    last = nc.vector.tensor_copy(
                        w_packed[:, 2 * SELF + kind, :, :, DK * term:DK * term + DK],
                        w_sb[:, ws[SELF], :].rearrange("p (j q k) -> p q j k", j=BLOCKS, q=QUADS))
            last.then_inc(weights_packed, 1)
            dve.wait_ge(pool_setup, N_POOL_SETUP)
            nc.vector.tensor_copy(ident_r[:, :], ident[:, :]).then_inc(dve_setup, 1)
            nc.vector.tensor_copy(ident_b[:, :], ident[:, :]).then_inc(dve_setup, 1)
            dve.wait_ge(bias_ps, 1)
            nc.vector.tensor_copy(flags[:, :], k_bank[:, 0:4]).then_inc(bias_done, 1)
            dve.wait_ge(rows_in, 16 * 3)
            for n in range(-LOAD_AHEAD, 1):
                step((None, n))
            for kind in range(2):
                for term in range(TERMS):
                    last = nc.vector.tensor_copy(
                        bias_row[0:1, kind, :, :, DK * term:DK * term + DK],
                        qk_bias_sb[0:1, kind, :].rearrange("p (j q k) -> p q j k", j=BLOCKS, q=QUADS))
            last.then_inc(bias_chain, 1)
            rest = bias_row[:, :, :, :, :].rearrange("p a q j r -> p (a q j r)")
            for part in range(BIAS_PARTS):
                dve.wait_ge(bias_chain, 2 * part + 1)
                rounded = bias_split[:, part, :, :, :].rearrange("p a q m -> p (a q m)")
                nc.vector.tensor_copy(rounded, rest).then_inc(bias_chain, 1)
                if part < BIAS_PARTS - 1:
                    dve.wait_ge(bias_chain, 2 * part + 2)
                    nc.vector.tensor_tensor(bias_rest[:, part, :], rest, rounded, ALU.subtract).then_inc(bias_chain, 1)
                    rest = bias_rest[:, part, :]
            run_steps(dve, step, 1, STREAM + 2)

        @block.gpsimd
        def _(pool):
            def attention_rstd(u):
                if not exists(u) or layer_of(u) == OUTER:
                    return
                pool.wait_ge(norm.sem, norm(u, 6))
                nc.gpsimd.tensor_tensor(rstd[:, :], var_eps[:, :], minus_half[:, :],
                                        ALU.pow).then_inc(rstd_ready.sem, 1)

            def tail_rstd(w):
                if not exists(w) or layer_of(w) == SELF:
                    return
                pool.wait_ge(tail_norm.sem, tail_norm(w, tail_norm.per[layer_of(w)] - 1))
                nc.gpsimd.tensor_tensor(rstd2[:, :], var_eps2[:, :], minus_half[:, :],
                                        ALU.pow).then_inc(rstd2_ready.sem, 1)

            def outer_inputs(u):
                if not exists(u) or layer_of(u) != OUTER:
                    return
                pool.wait_ge(norm.sem, norm(u))
                pool.wait_ge(tail_T_done.sem, tail_T_done(plus(u, -1)))
                nc.gpsimd.tensor_tensor(ctx_v[:, :], z[:, :], rows_sb[:, BV, :],
                                        ALU.add).then_inc(outer_ctx_ready.sem, 1)
                pool.wait_ge(tail_norm.sem, tail_norm(plus(u, -1)))
                pool.wait_ge(x3_ready.sem, x3_ready(plus(u, -TO_OUTER)))
                nc.gpsimd.tensor_tensor(tail_res[:, 1, :], x3[:, ring_of(u), :], rows_sb[:, BO, :],
                                        ALU.add).then_inc(outer_res_ready.sem, 1)

            def pack_q(f):
                if not exists(f):
                    return
                pool.wait_ge(q_sb_ready.sem, q_sb_ready(f))
                pool.wait_ge(high_q_ready.sem, high_q_ready(f))
                pool.wait_ge(attended.sem, attended(plus(f, -LAYERS)))
                pool.wait_ge(packed_k.sem, packed_k(f))
                nc.gpsimd.tensor_tensor(packed[:, layer_of(f), 0, :, :], q_sb[:, :, :],
                                        high_q[:, :, :].bitcast(F32), ALU.subtract).then_inc(packed_q.sem, 1)

            def spread_first(f):
                if not exists(f) or layer_of(f) == OUTER:
                    return
                pool.wait_ge(packed_q.sem, packed_q(f))
                pool.wait_ge(first_done.sem, first_done(plus(f, -1)))
                nc.gpsimd.tensor_tensor(
                    first_q[:, :].rearrange("p (q c) -> p q c", c=H + 1)[:, :, 0:H:QUADS],
                    packed[:, layer_of(f), 0, :, 0:1].bitcast(F32).broadcast_to([128, QUADS, BLOCKS]),
                    block_mask[:, :].unsqueeze(1).broadcast_to([128, QUADS, BLOCKS]),
                    ALU.mult).then_inc(first_ready.sem, 1)

            def step(u):
                outer_inputs(u)
                tail_rstd(plus(u, -1))
                attention_rstd(u)
                pack_q(plus(u, AHEAD))
                spread_first(plus(u, AHEAD))

            nc.gpsimd.memset(w_packed[:, :, :, :, :].rearrange("p a q j r -> p (a q j r)"), 0.0).then_inc(pool_zeros, 1)
            nc.gpsimd.memset(bias_row[:, :, :, :, :].rearrange("p a q j r -> p (a q j r)"), 0.0).then_inc(pool_zeros, 1)
            nc.gpsimd.memset(ident[:, :], 0.0).then_inc(pool_zeros, 1)
            nc.gpsimd.memset(future_s[:, :], 0.0).then_inc(pool_zeros, 1)
            nc.gpsimd.memset(future_t[:, :], 0.0).then_inc(pool_zeros, 1)
            nc.gpsimd.memset(flag_row[:, :, :, :].rearrange("p a j r -> p (a j r)"), 0.0).then_inc(pool_zeros, 1)
            nc.gpsimd.memset(block_mask[:, :], 0.0).then_inc(pool_zeros, 1)
            pool.wait_ge(pool_zeros, 7)
            setup = [0]

            def done(instruction):
                setup[0] += 1
                instruction.then_inc(pool_setup, 1)
                pool.wait_ge(pool_setup, setup[0])

            done(nc.gpsimd.memset(bias_row[0:1, 0, :, 0, SLEN_ROW:SLEN_ROW + 1], 1.0))
            done(nc.gpsimd.memset(bias_row[0:1, 1, :, 0, NEGMAX_ROW:NEGMAX_ROW + 2], 1.0))
            done(nc.gpsimd.memset(flag_row[0:1, 2, 0, SLEN_ROW:SLEN_ROW + 1], 1.0))
            done(nc.gpsimd.memset(flag_row[0:1, 3, 0, NEGMAX_ROW:NEGMAX_ROW + 2], 1.0))
            done(nc.gpsimd.memset(flag_row[0:1, 0, :, 2 * DK:3 * DK], 1.0))
            done(nc.gpsimd.memset(flag_row[0:1, 1, :, DK:2 * DK], 1.0))
            done(nc.gpsimd.memset(ones_b[:, :], 1.0))
            done(nc.gpsimd.memset(one_sb[:, :], 1.0))
            done(nc.gpsimd.memset(minus_half[:, :], -0.5))
            for j in range(BLOCKS):
                done(nc.gpsimd.memset(block_mask[ROWS * j:ROWS * j + ROWS, j:j + 1], 1.0))
            done(nc.gpsimd.affine_select(out=ident[:, :], in_=ident[:, :], compare_op=ALU.not_equal, fill=1.0, base=0,
                                         pattern=[[-1, 128]], channel_multiplier=1))
            done(nc.gpsimd.affine_select(out=future_s[:, :], in_=future_s[:, :], compare_op=ALU.is_ge, fill=-BIG,
                                         base=0, pattern=[[-1, S]], channel_multiplier=1))
            done(nc.gpsimd.affine_select(out=future_t[:, :], in_=future_t[:, :], compare_op=ALU.is_ge, fill=-BIG,
                                         base=0, pattern=[[1, S]], channel_multiplier=-1))
            done(nc.gpsimd.iota(iota_t[:, :], pattern=[[1, S]], base=0, channel_multiplier=0,
                                allow_small_or_imprecise_dtypes=True))
            done(nc.gpsimd.memset(first_q[:, :], 0.0))

            def clear_spread(l):
                if l != SELF:
                    nc.gpsimd.memset(spread[:, l, :, :, :, :].rearrange("p a j q s -> p (a j q s)").bitcast(F32),
                                     0.0).then_inc(zeroed[l], 1)
                pool.wait_ge(zeroed[l], 1)
                view = spread[0:ROWS, l, 0, :, :, :].rearrange("p j q s -> p j (q s)")
                nc.gpsimd.affine_select(out=view, in_=view.bitcast(F32), compare_op=ALU.not_equal, fill=1.0,
                                        base=-TLEN_ROW, pattern=[[-1, BLOCKS], [0, QUADS * S]],
                                        channel_multiplier=1).then_inc(zeroed[l], 1)

            clear_spread(SELF)
            for n in range(-LOAD_AHEAD, 1 - AHEAD):
                step((None, n))
            clear_spread(CROSS)
            clear_spread(OUTER)
            run_steps(pool, step, 1 - AHEAD, STREAM + 2)

        @block.sync
        def _(sp):
            def row_of(unit):
                turn, m = unit[0], sequence_of(unit)
                return slice(m, m + 1) if turn is None else bass.ds(sp.snap(turn * RING + m), 1)

            def load(v):
                if not exists(v) or layer_of(v) == OUTER:
                    return
                r = ring_of(v)
                if layer_of(v) == SELF:
                    at = row_of(v)
                    sp.wait_ge(norm.sem, norm(plus(v, -PERIOD), 3))
                    sp.dma_start(x_in[:, r, :], x[at, :, :].rearrange("o s d -> (o s) d")).then_inc(x_loaded[r].sem, 16)
                else:
                    at = row_of(v)
                    sp.wait_ge(x_T_done.sem, x_T_done(plus(v, TO_OUTER - PERIOD)))
                    sp.dma_start(ctx[:, r, :], ctx_in[at, :, :].rearrange("o s d -> (o s) d")).then_inc(
                        ctx_loaded[r].sem, 16)

            def put_negmax(u):
                if not exists(u):
                    return
                l = layer_of(u)
                sp.wait_ge(negmax_T_ready.sem, negmax_T_ready(u))
                sp.dma_start(spread[NEGMAX_ROW:NEGMAX_ROW + 2, l, 0, :, :, :].rearrange("p j q s -> p (j q) s").bitcast(F32),
                             negmax_T[:, :].bitcast(F32)).then_inc(negmax_done[l].sem, 16)

            def put_spread(f):
                if not exists(f):
                    return
                l = layer_of(f)
                sp.wait_ge(packed_q.sem, packed_q(f))
                if f[0] is None:
                    sp.wait_ge(zeroed[l], 2)
                for j in range(BLOCKS):
                    at = slice(ROWS * j, ROWS * j + DATA)
                    sp.dma_start(spread[at, l, :, j, :, :].bitcast(F32),
                                 packed[at, l, :, :, :].bitcast(F32)).then_inc(spread_done[l].sem, 16)

            def put_length(f, part):
                if not exists(f) or layer_of(f) == OUTER:
                    return
                l = layer_of(f)
                if part == 0:
                    sp.wait_ge(len_chain.sem, len_chain(f))
                    dst = spread[SLEN_ROW:SLEN_ROW + 1, l, 1, :, :, :].rearrange("p j q s -> p (j q) s")
                else:
                    dst = packed[TLEN_ROW:TLEN_ROW + BLOCKS, l, 1, :, :]
                sp.dma_start(dst.bitcast(F32), len_mask[:, l, :].bitcast(F32)).then_inc(len_done[l].sem, 16)

            def store(w):
                if not exists(w) or layer_of(w) != OUTER:
                    return
                r, at = ring_of(w), row_of(w)
                sp.wait_ge(y_ready.sem, y_ready(w))
                sp.dma_start(out[at, :, :].rearrange("o s d -> (o s) d"), y_out[:, r, :]).then_inc(out_stored[r].sem, 16)

            def step(u):
                put_spread(plus(u, AHEAD - 1))
                put_length(plus(u, AHEAD - 1), 0)
                put_negmax(plus(u, 1))
                put_length(plus(u, AHEAD - 1), 1)
                store(plus(u, -2))
                load(plus(u, LOAD_AHEAD))

            sp.dma_start(w_sb[:, 0:LAYERS, :], weights[:, 0:LAYERS, :]).then_inc(weights_in, 16)
            sp.dma_start(w_sb[:, LAYERS:N_WEIGHTS, :], weights[:, LAYERS:N_WEIGHTS, :]).then_inc(weights_in_2, 16)
            sp.dma_start(qk_bias_sb[:, :, :], qk_bias).then_inc(rows_in, 16)
            sp.dma_start(fc1_bias_sb[:, :], fc1_bias).then_inc(rows_in, 16)
            sp.dma_start(rows_sb[:, :, :], rows.unsqueeze(0).broadcast_to([128, N_ROWS, D])).then_inc(rows_in, 16)
            for n in range(-LOAD_AHEAD, 1 - AHEAD):
                step((None, n))
            for n in range(1 - AHEAD, 2):
                step((None, n))
            sp.wait_ge(bias_chain, 2 * BIAS_PARTS)
            sp.dma_start(bias_parts[:, :, :, :].rearrange("p a q m -> p (a q m)"),
                         bias_split[:, :, :, :, :].rearrange("p n a q m -> p n (a q m)")).then_inc(bias_in, 16)
            run_steps(sp, step, 2, STREAM + 2)
            for r in range(RING):
                sp.wait_ge(out_stored[r].sem, out_stored[r]((None, STREAM)))


def kernel(x, ctx_1024, L0_xattn_Wq1, L0_xattn_Wk1, L0_xattn_Wv1, L0_xattn_Wq2, L0_xattn_Wk2, L0_xattn_Wv2,
           L0_xattn_ln1_g, L0_xattn_ln1_b, L0_xattn_ln2_g, L0_xattn_ln2_b, L0_xattn_ln3_g, L0_xattn_ln3_b,
           L0_xattn_fc1_w, L0_xattn_fc1_b, L0_xattn_fc2_w, L0_xattn_fc2_b, L1_xattn_W_qkv, L1_xattn_b_qkv,
           L1_xattn_W_o, L1_xattn_b_o, L1_xattn_ln_gamma, L1_xattn_ln_beta):
    import numpy as np
    from concourse import bacc
    from concourse.bass_utils import run_bass_kernel_spmd

    def heads_last(w):
        return np.asarray(w).transpose(1, 0, 2).reshape(D, D)

    qkv = np.asarray(L1_xattn_W_qkv).reshape(3, D, D)
    qkv_bias = np.asarray(L1_xattn_b_qkv).reshape(3, D)
    weights = np.stack(
        [heads_last(w) for w in (L0_xattn_Wq1, L0_xattn_Wk1, L0_xattn_Wv1, L0_xattn_Wq2, L0_xattn_Wk2, L0_xattn_Wv2)]
        + [np.asarray(w).T for w in (qkv[0], qkv[1], qkv[2], L1_xattn_W_o, L0_xattn_fc1_w, L0_xattn_fc2_w)], axis=1)
    rows = np.stack([np.asarray(r) for r in (
        L0_xattn_ln1_g, L0_xattn_ln1_b, L0_xattn_ln2_g, L0_xattn_ln2_b, L0_xattn_ln3_g, L0_xattn_ln3_b,
        L0_xattn_fc2_b, L1_xattn_ln_gamma, L1_xattn_ln_beta, L1_xattn_b_o, qkv_bias[2])])
    arrays = {
        "x": np.asarray(x), "ctx": np.asarray(ctx_1024), "weights": np.ascontiguousarray(weights),
        "rows": rows, "qk_bias": np.ascontiguousarray(qkv_bias[0:2]).reshape(1, 2, D),
        "fc1_bias": np.asarray(L0_xattn_fc1_b).reshape(D, 1),
    }
    nc = bacc.Bacc("TRN2", target_bir_lowering=False, num_devices=1)
    ins = [nc.dram_tensor(f"{name}_dram", a.shape, mybir.dt.from_np(a.dtype), kind="ExternalInput").ap()
           for name, a in arrays.items()]
    out = nc.dram_tensor("out_dram", (B, S, D), F32, kind="ExternalOutput").ap()
    xattn_kernel(nc, *ins, out)
    got = run_bass_kernel_spmd(nc, [{f"{name}_dram": a for name, a in arrays.items()}], core_ids=[0])
    return got.results[0]["out_dram"]
```
